# Optimizing a Trainium2 kernel written in Bass

```python
import numpy as np
import jax
import jax.numpy as jnp

def _softmax(x, axis=-1):
    return jax.nn.softmax(x, axis=axis)

def _gelu(x):
    return jax.nn.gelu(x, approximate=True)

def _silu(x):
    return jax.nn.silu(x)

def _sigmoid(x):
    return jax.nn.sigmoid(x)

def _layernorm(x, axis=-1, eps=1e-05):
    m = jnp.mean(x, axis=axis, keepdims=True)
    v = jnp.var(x, axis=axis, keepdims=True)
    return (x - m) / jnp.sqrt(v + eps)

def _scatter_add(tgt, idx, src, axis=0):
    return tgt.at[idx].add(src)

def _segment_sum(src, seg, n):
    return jax.ops.segment_sum(src, seg, n)
kernel_name = 'mk_adaln_ffn_d1_seqx_r2_6159af'

def setup_inputs(seed: int=0):
    np.random.seed(seed)
    _w = jnp.asarray

    def _rec_inputs():
        import jax
        import jax.numpy as jnp
        _rk = jax.random.key(seed)
        x = -0.000125 + 0.9999 * jax.random.normal(jax.random.fold_in(_rk, 1), (4, 1024, 1024), jnp.float32)
        _lenS = 1024 - jax.random.randint(jax.random.fold_in(_rk, 7), (4,), 0, max(1, 1024 // 4) + 1, jnp.int32)
        _lenS2 = 1024 - jax.random.randint(jax.random.fold_in(_rk, 8), (4,), 0, max(1, 1024 // 4) + 1, jnp.int32)
        fside_BxSxS_0 = -1.52775e-05 + 0.999936 * jax.random.normal(jax.random.fold_in(_rk, 11), (4, 1024, 1024), jnp.float32)
        cond_512 = -5.03954e-05 + 1.00559 * jax.random.normal(jax.random.fold_in(_rk, 12), (4, 256), jnp.float32)
        return (x, fside_BxSxS_0, cond_512)
    x, fside_BxSxS_0, cond_512 = _rec_inputs()

    def _L0_cond_setup():
        import jax, jax.numpy as jnp
        from jax import lax
        import numpy as np
        B, T, C, TD = (8, 1024, 1024, 256)

        def _bi_wkv(r, k, v, w, u, time_emb):
            tf = jax.nn.sigmoid(jnp.sum(time_emb, axis=-1))[:, None, None]
            decay = jnp.exp(-jnp.exp(w.astype(jnp.float32)))[None, :] * (0.5 + 0.5 * tf[:, :, 0])
            kf = k.astype(jnp.float32)
            vf = v.astype(jnp.float32)
            ek = jnp.exp(jnp.minimum(kf, 30.0))
            ekv = ek * vf

            def step(carry, x):
                a, b = carry
                ekv_t, ek_t = x
                a = a * decay + ekv_t
                b = b * decay + ek_t
                return ((a, b), (a, b))
            ekv_t = jnp.swapaxes(ekv, 0, 1)
            ek_t = jnp.swapaxes(ek, 0, 1)
            init = (jnp.zeros_like(decay), jnp.zeros_like(decay))
            _, (nf, df) = lax.scan(step, init, (ekv_t, ek_t))
            _, (nb, db) = lax.scan(step, init, (ekv_t, ek_t), reverse=True)
            nf = jnp.swapaxes(nf, 0, 1)
            df = jnp.swapaxes(df, 0, 1)
            nb = jnp.swapaxes(nb, 0, 1)
            db = jnp.swapaxes(db, 0, 1)
            euk = jnp.exp(jnp.minimum(u.astype(jnp.float32)[None, None, :] + kf, 30.0))
            num = nf + nb - ekv + euk * vf
            den = df + db - ek + euk
            base = jax.nn.sigmoid(r.astype(jnp.float32)) * (num / jnp.maximum(den, 1e-08))
            out = base * (0.8 + 0.2 * tf)
            return out.astype(r.dtype)
        key = jax.random.key(seed)
        ks = jax.random.split(key, 6)
        return {'r': jax.random.normal(ks[0], (B, T, C), dtype=jnp.float32), 'k': jax.random.normal(ks[1], (B, T, C), dtype=jnp.float32), 'v': jax.random.normal(ks[2], (B, T, C), dtype=jnp.float32), 'w': jax.random.normal(ks[3], (C,), dtype=jnp.float32), 'u': jax.random.normal(ks[4], (C,), dtype=jnp.float32), 'time_emb': jax.random.normal(ks[5], (B, TD), dtype=jnp.float32)}
    _L0_cond_all = _L0_cond_setup()
    _L0_cond_in = {k: v for k, v in _L0_cond_all.items() if k in ('w', 'u')}
    del _L0_cond_all

    def _L0_ffn_setup():
        import jax, jax.numpy as jnp
        import numpy as np
        B, L, D = (4, 1024, 1024)
        S, K, NB = (16, 4, 2)
        H = D // 64
        EPS = 1e-06

        def _rms(x, w):
            return x * jax.lax.rsqrt(jnp.mean(x * x, axis=-1, keepdims=True) + EPS) * w
        key = jax.random.key(seed)
        ks = jax.random.split(key, 8)
        g = lambda k, shape, s: jax.random.normal(k, shape, dtype=jnp.float32) * s
        return {'x': g(ks[0], (B, L, D), 1.0), 'workspace': g(ks[1], (S, D), 0.02), 'compete_w': g(ks[2], (S, D), 0.02), 'compete_b': jnp.zeros((S,), jnp.float32), 'write_w': g(ks[3], (D, D), 0.02), 'write_b': jnp.zeros((D,), jnp.float32), 'in_proj_w': g(ks[4], (3 * D, D), 0.02), 'in_proj_b': jnp.zeros((3 * D,), jnp.float32), 'out_proj_w': g(ks[5], (D, D), 0.02), 'out_proj_b': jnp.zeros((D,), jnp.float32), 'ig_w': g(ks[6], (1, D), 0.02), 'ig_b': jnp.zeros((1,), jnp.float32), 'norm_pre_w': jnp.ones((D,), jnp.float32), 'norm_post_w': jnp.ones((D,), jnp.float32)}
    _L0_ffn_all = _L0_ffn_setup()
    _L0_ffn_in = {k: v for k, v in _L0_ffn_all.items() if k in ('workspace', 'compete_w', 'compete_b', 'write_w', 'write_b', 'in_proj_w', 'in_proj_b', 'out_proj_w', 'out_proj_b', 'ig_w', 'ig_b', 'norm_pre_w', 'norm_post_w')}
    del _L0_ffn_all
    return {'x': x, 'fside_BxSxS_0': fside_BxSxS_0, 'cond_512': cond_512, 'L0_cond_w': _L0_cond_in['w'], 'L0_cond_u': _L0_cond_in['u'], 'L0_ffn_workspace': _L0_ffn_in['workspace'], 'L0_ffn_compete_w': _L0_ffn_in['compete_w'], 'L0_ffn_compete_b': _L0_ffn_in['compete_b'], 'L0_ffn_write_w': _L0_ffn_in['write_w'], 'L0_ffn_write_b': _L0_ffn_in['write_b'], 'L0_ffn_in_proj_w': _L0_ffn_in['in_proj_w'], 'L0_ffn_in_proj_b': _L0_ffn_in['in_proj_b'], 'L0_ffn_out_proj_w': _L0_ffn_in['out_proj_w'], 'L0_ffn_out_proj_b': _L0_ffn_in['out_proj_b'], 'L0_ffn_ig_w': _L0_ffn_in['ig_w'], 'L0_ffn_ig_b': _L0_ffn_in['ig_b'], 'L0_ffn_norm_pre_w': _L0_ffn_in['norm_pre_w'], 'L0_ffn_norm_post_w': _L0_ffn_in['norm_post_w']}

def reference(x, fside_BxSxS_0, cond_512, L0_cond_w, L0_cond_u, L0_ffn_workspace, L0_ffn_compete_w, L0_ffn_compete_b, L0_ffn_write_w, L0_ffn_write_b, L0_ffn_in_proj_w, L0_ffn_in_proj_b, L0_ffn_out_proj_w, L0_ffn_out_proj_b, L0_ffn_ig_w, L0_ffn_ig_b, L0_ffn_norm_pre_w, L0_ffn_norm_post_w):
    import jax
    import jax.numpy as jnp

    def _L0_cond_ref(r, k, v, w, u, time_emb):
        import jax, jax.numpy as jnp
        from jax import lax
        import numpy as np
        B, T, C, TD = (8, 1024, 1024, 256)

        def _bi_wkv(r, k, v, w, u, time_emb):
            tf = jax.nn.sigmoid(jnp.sum(time_emb, axis=-1))[:, None, None]
            decay = jnp.exp(-jnp.exp(w.astype(jnp.float32)))[None, :] * (0.5 + 0.5 * tf[:, :, 0])
            kf = k.astype(jnp.float32)
            vf = v.astype(jnp.float32)
            ek = jnp.exp(jnp.minimum(kf, 30.0))
            ekv = ek * vf

            def step(carry, x):
                a, b = carry
                ekv_t, ek_t = x
                a = a * decay + ekv_t
                b = b * decay + ek_t
                return ((a, b), (a, b))
            ekv_t = jnp.swapaxes(ekv, 0, 1)
            ek_t = jnp.swapaxes(ek, 0, 1)
            init = (jnp.zeros_like(decay), jnp.zeros_like(decay))
            _, (nf, df) = lax.scan(step, init, (ekv_t, ek_t))
            _, (nb, db) = lax.scan(step, init, (ekv_t, ek_t), reverse=True)
            nf = jnp.swapaxes(nf, 0, 1)
            df = jnp.swapaxes(df, 0, 1)
            nb = jnp.swapaxes(nb, 0, 1)
            db = jnp.swapaxes(db, 0, 1)
            euk = jnp.exp(jnp.minimum(u.astype(jnp.float32)[None, None, :] + kf, 30.0))
            num = nf + nb - ekv + euk * vf
            den = df + db - ek + euk
            base = jax.nn.sigmoid(r.astype(jnp.float32)) * (num / jnp.maximum(den, 1e-08))
            out = base * (0.8 + 0.2 * tf)
            return out.astype(r.dtype)
        return _bi_wkv(r, k, v, w, u, time_emb)

    def _L0_ffn_ref(x, workspace, compete_w, compete_b, write_w, write_b, in_proj_w, in_proj_b, out_proj_w, out_proj_b, ig_w, ig_b, norm_pre_w, norm_post_w):
        import jax, jax.numpy as jnp
        import numpy as np
        B, L, D = (4, 1024, 1024)
        S, K, NB = (16, 4, 2)
        H = D // 64
        EPS = 1e-06

        def _rms(x, w):
            return x * jax.lax.rsqrt(jnp.mean(x * x, axis=-1, keepdims=True) + EPS) * w
        Bq, Lq, Dd = x.shape
        hd = Dd // H
        scale = 1.0 / np.sqrt(hd).astype(np.float32)
        ws = jnp.broadcast_to(workspace[None], (Bq, S, Dd))
        wq, wk, wv = (in_proj_w[:Dd], in_proj_w[Dd:2 * Dd], in_proj_w[2 * Dd:])
        bq, bk, bv = (in_proj_b[:Dd], in_proj_b[Dd:2 * Dd], in_proj_b[2 * Dd:])
        k_eff = min(K, Lq)
        for _ in range(NB):
            logits = _rms(x, norm_pre_w) @ compete_w.T + compete_b
            slot_logits = jnp.swapaxes(logits, 1, 2)
            vals, idx = jax.lax.top_k(slot_logits, k_eff)
            wgt = jax.nn.softmax(vals, axis=-1)
            wx = x @ write_w.T + write_b
            gathered = jnp.take_along_axis(wx[:, None], idx[..., None], axis=2)
            written = jnp.einsum('bsk,bskd->bsd', wgt, gathered)
            ws = _rms(ws + written, norm_post_w)
            q = (x @ wq.T + bq).reshape(Bq, Lq, H, hd)
            kk = (ws @ wk.T + bk).reshape(Bq, S, H, hd)
            vv = (ws @ wv.T + bv).reshape(Bq, S, H, hd)
            att = jax.nn.softmax(jnp.einsum('blhd,bshd->bhls', q, kk) * scale, axis=-1)
            ctx = jnp.einsum('bhls,bshd->blhd', att, vv).reshape(Bq, Lq, Dd)
            x_b = ctx @ out_proj_w.T + out_proj_b
            x = _rms(x + x_b, norm_post_w)
            ignition = jax.nn.sigmoid(x @ ig_w.T + ig_b)
        return x
    x = x + _L0_ffn_ref(_L0_cond_ref(x, fside_BxSxS_0, fside_BxSxS_0, L0_cond_w, L0_cond_u, cond_512), L0_ffn_workspace, L0_ffn_compete_w, L0_ffn_compete_b, L0_ffn_write_w, L0_ffn_write_b, L0_ffn_in_proj_w, L0_ffn_in_proj_b, L0_ffn_out_proj_w, L0_ffn_out_proj_b, L0_ffn_ig_w, L0_ffn_ig_b, L0_ffn_norm_pre_w, L0_ffn_norm_post_w)
    return x

_drawn_inputs = setup_inputs


def setup_inputs(seed=0):
    import zlib

    import numpy as np

    out = dict(_drawn_inputs(seed))
    spreads = {'L0_ffn_compete_b': (0.0, 0.8),
     'L0_ffn_write_b': (0.0, 0.1),
     'L0_ffn_in_proj_b': (0.0, 0.1),
     'L0_ffn_out_proj_b': (0.0, 0.1),
     'L0_ffn_norm_pre_w': (1.0, 0.2),
     'L0_ffn_norm_post_w': (1.0, 0.2)}
    factors = {'L0_ffn_workspace': 4.086}
    for name, (base, spread) in spreads.items():
        noise = np.random.default_rng([zlib.crc32(name.encode()), seed]).standard_normal(out[name].shape)
        drawn = base * np.exp(spread * noise) if base else spread * noise
        out[name] = jnp.asarray(drawn.astype(out[name].dtype))
    for name, factor in factors.items():
        out[name] = (out[name] * factor).astype(out[name].dtype)
    return out
```

```python
import concourse.bass as bass
from concourse import mybir
from contextlib import ExitStack

fp32 = mybir.dt.float32
bf16 = mybir.dt.bfloat16
ALU = mybir.AluOpType
ACT = mybir.ActivationFunctionType
AXX = mybir.AxisListType.X

P = 128
B, T, C = 4, 1024, 1024
TD = 256
S, K = 16, 4
H = C // 64
NC = C // P
NT = B * NC
BS = B * S
HS = H * S
HP = H // 2
Q = 4
TQ = T // Q
EXP_CAP = 10686474581524.463
ER_CAP = 2.0 ** 62
BIG = 3.0e38
SCALE = 0.125


def wait(eng, sem, count):
    if not (isinstance(count, int) and count <= 0):
        eng.wait_ge(sem, count)


def exists(n):
    return not isinstance(n, int) or 0 <= n < NT


def over_tiles(eng, body, lag):
    fill = 2 * ((lag + 1) // 2) or 2
    for n in range(fill):
        body(n, n % 2)
    with eng.Fori(fill // 2, NT // 2 - 1) as j:
        for p in range(2):
            body(j * 2 + p, p)
    for n in range(NT - 2, NT + lag):
        body(n, n % 2)


def build(nc, xT, kT, x, cond, w_cols, u_cols, work_t, cw_cols, npre_cols, cb_col, wr_T, wr_b, wq, wk_T,
          wv_T, bq_cols, bk_cols, bv_cols, wo_T, wo_b, npost, out):
    with ExitStack() as ctx:
        def sb(name, shape, dt=fp32):
            return ctx.enter_context(nc.sbuf_tensor(name, shape, dt))

        def sem(name):
            return ctx.enter_context(nc.semaphore(name))

        x0T_d = nc.dram_tensor("x0T_scratch", [NT, P, T], fp32).ap()
        x1T_d = nc.dram_tensor("x1T_scratch", [NT, P, C], fp32).ap()
        A_d = nc.dram_tensor("A_scratch", [B, HP, P, NC * 32], fp32).ap()
        Bm_d = nc.dram_tensor("B_scratch", [B, 2, P, C], fp32).ap()
        sb_d = nc.dram_tensor("score_bias_scratch", [HP, B, 32], fp32).ap()

        xres = sb("xres", [P, NT, NC, P])
        ident = sb("ident", [P, P])
        cwz = sb("cwz", [P, NC, 32])
        cws = sb("cws", [P, 2, 32])
        sumsq_w = sb("sumsq_w", [P, 32])
        fold = sb("fold", [P, S])
        rows = sb("rows", [P, P])
        ones_row, head0_row = rows[0:1, :], [rows[64:65, :], rows[96:97, :]]
        tiny = sb("tiny", [P, 4])
        decay = sb("decay", [P, B, NC])
        gain = sb("gain", [P, B, NC])
        ucol = sb("ucol", [P, NT])
        wcol = sb("wcol", [P, NT])
        small = sb("small", [P, 32])
        cbcol = sb("cbcol", [BS, 1])
        bqc = sb("bqc", [P, HP])
        bkc = sb("bkc", [P, HP])
        bvc = sb("bvc", [P, HP])
        nprec = sb("nprec", [P, NC])
        top8 = sb("top8", [BS, 24])
        hstat = sb("hstat", [P, 4])
        work = sb("work", [P, 18944])

        def cut(at, n):
            return work[:, at:at + n]

        banks = [ctx.enter_context(nc.psum_tensor(f"bank{i}", [P, 2 * 512], fp32)) for i in range(4)]

        cin = sem("const_in")
        c_id = sem("const_ident")
        c_dve = sem("const_dve")
        c_act = sem("const_act")
        condb = cut(0, B * TD)
        cwraw = cut(1024, NC * S)
        with nc.Block() as block:
            @block.sync
            def _(sp):
                sp.dma_start(condb.rearrange("p (b d) -> p b d", b=B),
                             cond.rearrange("(o b) d -> o b d", o=1).broadcast_to([P, B, TD])).then_inc(cin, 16)
                for dst, src in ((wcol[:], w_cols), (ucol[:], u_cols), (cwraw, cw_cols), (nprec[:], npre_cols),
                                 (cbcol[:], cb_col), (bqc[:], bq_cols), (bkc[:], bk_cols), (bvc[:], bv_cols)):
                    sp.dma_start(dst, src).then_inc(cin, 16)

            @block.gpsimd
            def _(pool):
                nc.gpsimd.memset(ident[:], 0.0).then_inc(c_id, 1)
                nc.gpsimd.memset(fold[:], 0.0).then_inc(c_id, 1)
                nc.gpsimd.memset(ones_row, 1.0).then_inc(c_id, 1)
                pool.wait_ge(c_id, 3)
                nc.gpsimd.affine_select(out=ident[:], in_=ident[:], compare_op=ALU.not_equal, fill=1.0, base=0,
                                        pattern=[[-1, P]], channel_multiplier=1).then_inc(c_id, 1)
                for q in range(Q):
                    nc.gpsimd.affine_select(out=fold[:], in_=fold[:], compare_op=ALU.not_equal, fill=1.0,
                                            base=-32 * q, pattern=[[-1, S]], channel_multiplier=1).then_inc(c_id, 1)
                    pool.wait_ge(c_id, 5 + q)

            @block.vector
            def _(dve):
                n = [0]

                def step(ins):
                    n[0] += 1
                    ins.then_inc(c_dve, 1)
                    dve.wait_ge(c_dve, n[0])

                step(nc.vector.memset(tiny[:, 0:1], -1e-8))
                step(nc.vector.memset(tiny[:, 1:2], 1e-8))
                step(nc.vector.memset(tiny[:, 2:4], 1e-6))
                step(nc.vector.memset(cwz[:], 0.0))
                step(nc.vector.memset(sumsq_w[:], 0.0))
                step(nc.vector.memset(sumsq_w[:, S:S + 1], 1.0))
                step(nc.vector.memset(head0_row[0], 0.0))
                step(nc.vector.memset(head0_row[0].rearrange("o (b r) -> o b r", b=B)[:, :, 0:S], 1.0))
                step(nc.vector.memset(top8[:, 8:16], BIG))
                dve.wait_ge(cin, 9 * 16)
                step(nc.vector.tensor_reduce(small[:, 0:4], condb.rearrange("p (b d) -> p b d", b=B), AXX, ALU.add))
                step(nc.vector.tensor_tensor(cwz[:, :, 0:S], cwraw.rearrange("p (c s) -> p c s", c=NC),
                                             nprec[:].rearrange("p (c o) -> p c o", o=1).broadcast_to([P, NC, S]),
                                             ALU.mult))
                dve.wait_ge(c_act, 3)
                step(nc.vector.tensor_scalar(small[:, 8:12], small[:, 4:8], 1.0, None, ALU.add))
                step(nc.vector.reciprocal(small[:, 12:16], small[:, 8:12]))
                step(nc.vector.tensor_scalar(small[:, 16:20], small[:, 12:16], 0.5, 0.5, ALU.mult, ALU.add))
                step(nc.vector.tensor_scalar(small[:, 20:24], small[:, 12:16], 0.2, 0.8, ALU.mult, ALU.add))
                half = small[:, 16:20].rearrange("p (b o) -> p b o", o=1).broadcast_to([P, B, NC])
                g4 = small[:, 20:24].rearrange("p (b o) -> p b o", o=1).broadcast_to([P, B, NC])
                step(nc.vector.tensor_tensor(decay[:], wcol[:].rearrange("p (b c) -> p b c", b=B), half, ALU.mult))
                step(nc.vector.tensor_copy(gain[:], g4))
                step(nc.vector.memset(head0_row[1], 0.0))
                step(nc.vector.memset(head0_row[1].rearrange("o (b r) -> o b r", b=B)[:, :, 0:S], 1.0))

            @block.scalar
            def _(act):
                nc.scalar.preload_act_table_set("natural_log_exp_and_others")
                act.wait_ge(cin, 9 * 16)
                nc.scalar.activation(wcol[:], wcol[:], ACT.Exp).then_inc(c_act, 1)
                act.wait_ge(c_act, 1)
                nc.scalar.activation(wcol[:], wcol[:], ACT.Exp, scale=-1.0).then_inc(c_act, 1)
                act.wait_ge(c_dve, 10)
                nc.scalar.activation(small[:, 4:8], small[:, 0:4], ACT.Exp, scale=-1.0).then_inc(c_act, 1)

        kbuf = [cut(1024 * i, T) for i in (0, 1)]
        rbuf = [cut(1024 * i, T) for i in (2, 9)]
        ekr = cut(3072, T)
        ek = cut(4096, T)
        ekv = cut(5120, T)
        eur = cut(6144, T)
        delta = [cut(1024 * i, T) for i in (7, 8)]
        nf = cut(10240, T)
        nb = cut(11264, T)
        den = [cut(1024 * i, T) for i in (12, 13)]
        db = cut(14336, T)
        x0T = cut(15360, T)
        sq = cut(16384, T)
        lgacc = cut(17408, B * TQ).rearrange("p (b t) -> p b t", b=B)
        ps_num = banks[0:2]
        ps_nat = banks[2]
        ps_lg = banks[3]

        cond_sems = []
        cond_ctx = ExitStack()

        def csem(name):
            cond_sems.append(cond_ctx.enter_context(nc.semaphore(name)))
            return cond_sems[-1]

        k_in = [csem("k_in_even"), csem("k_in_odd")]
        r_in = [csem("r_in_even"), csem("r_in_odd")]
        x0_out = csem("x0_out")
        ek_raw, eu_raw, er_raw = csem("ek_raw"), csem("eu_raw"), csem("er_raw")
        ek_ok, er_ok, ekv_ok, delta_ok = csem("ek_ok"), csem("er_ok"), csem("ekv_ok"), csem("delta_ok")
        df_ok, db_ok, nf_ok, nb_ok = csem("df_ok"), csem("db_ok"), csem("nf_ok"), csem("nb_ok")
        dv_ok, sum1_ok, den_ok = csem("dv_ok"), csem("sum1_ok"), csem("den_ok")
        l1_ok, guard_ok, l2_ok, s_ok, y_ok = csem("l1_ok"), csem("guard_ok"), csem("l2_ok"), csem("s_ok"), csem("y_ok")
        num_ok, x0_ok, sq_ok, cws_ok = csem("num_ok"), csem("x0_ok"), csem("sq_ok"), csem("cws_ok")
        nat_ok, nat_ev, lg_ok, lg_add = csem("nat_ok"), csem("nat_ev"), csem("lg_ok"), csem("lg_add")
        dv_used, lg_zero = csem("dv_used"), csem("lg_zero")

        with nc.Block() as block:
            @block.sync
            def _(sp):
                def load_k(n, p):
                    wait(sp, dv_used, n - 1)
                    sp.dma_start(kbuf[p], kT[n, :, :]).then_inc(k_in[p], 16)

                load_k(0, 0)

                def body(n, p):
                    if exists(n + 1):
                        load_k(n + 1, 1 - p)
                    if exists(n):
                        wait(sp, s_ok, n - 1)
                        sp.dma_start(rbuf[p], xT[n, :, :]).then_inc(r_in[p], 16)
                    if exists(n - 2):
                        wait(sp, x0_ok, n - 1)
                        sp.dma_start(x0T_d[n - 2, :, :], x0T).then_inc(x0_out, 16)

                over_tiles(sp, body, 2)
                sp.wait_ge(x0_out, 16 * NT)

            @block.scalar
            def _(act):
                act.wait_ge(c_dve, 19)

                def exps(n, p):
                    wait(act, k_in[p], (n // 2 + 1) * 16)
                    wait(act, ek_ok, n)
                    nc.scalar.activation(ekr, kbuf[p], ACT.Exp).then_inc(ek_raw, 1)
                    wait(act, delta_ok, n)
                    nc.scalar.activation(eur, kbuf[p], ACT.Exp, bias=ucol[:, bass.ds(n, 1)]).then_inc(eu_raw, 1)

                nc.scalar.preload_act_table_set("natural_log_exp_and_others")
                exps(0, 0)

                def body(n, p):
                    if exists(n - 2):
                        wait(act, x0_ok, n - 1)
                        wait(act, lg_ok, n - 2)
                        nc.scalar.activation(sq, x0T, ACT.Square).then_inc(sq_ok, 1)
                        nc.scalar.activation(cws[:, p, :], cwz[:, (n - 2) % NC, :], ACT.Copy).then_inc(cws_ok, 1)
                    if exists(n - 1):
                        wait(act, er_ok, n)
                        nc.scalar.activation(rbuf[1 - p], rbuf[1 - p], ACT.Ln, bias=1.0).then_inc(l1_ok, 1)
                        wait(act, den_ok, n)
                        d = den[1 - p]
                        nc.scalar.activation(d, d, ACT.Relu, bias=tiny[:, 0:1]).then_inc(guard_ok, 1)
                        wait(act, guard_ok, n)
                        nc.scalar.activation(d, d, ACT.Ln, bias=tiny[:, 1:2]).then_inc(l2_ok, 1)
                    if exists(n):
                        wait(act, r_in[p], (n // 2 + 1) * 16)
                        nc.scalar.activation(rbuf[p], rbuf[p], ACT.Exp, scale=-1.0).then_inc(er_raw, 1)
                    if exists(n + 1):
                        exps(n + 1, 1 - p)
                    if exists(n - 1):
                        wait(act, s_ok, n)
                        nc.scalar.activation(den[1 - p], den[1 - p], ACT.Exp, scale=-1.0).then_inc(y_ok, 1)
                    if exists(n - 2):
                        wait(act, nat_ok, n - 1)
                        nc.scalar.activation(xres[:, n - 2, :, :].rearrange("p a c -> p (a c)"), ps_nat[:, :],
                                             ACT.Copy).then_inc(nat_ev, 1)

                over_tiles(act, body, 2)

            @block.vector
            def _(dve):
                nc.vector.memset(lgacc, 0.0).then_inc(lg_zero, 1)

                def body(n, p):
                    if exists(n):
                        wait(dve, ek_raw, n + 1)
                        wait(dve, db_ok, n)
                        nc.vector.tensor_scalar(ek, ekr, EXP_CAP, None, ALU.min).then_inc(ek_ok, 1)
                        wait(dve, ek_ok, n + 1)
                        wait(dve, nb_ok, n)
                        nc.vector.tensor_tensor(ekv, ek, kbuf[p], ALU.mult).then_inc(ekv_ok, 1)
                        wait(dve, eu_raw, n + 1)
                        wait(dve, den_ok, n - 1)
                        nc.vector.scalar_tensor_tensor(delta[p], eur, EXP_CAP, ek, ALU.min, ALU.subtract)\
                            .then_inc(delta_ok, 1)
                        dec = decay[:].rearrange("p b c -> p (b c)")[:, bass.ds(n, 1)].broadcast_to([P, T])
                        wait(dve, x0_ok, n - 1)
                        nc.vector.tensor_tensor_scan(den[p], dec, ek, 0.0, ALU.mult, ALU.add).then_inc(df_ok, 1)
                        wait(dve, sum1_ok, n)
                        nc.vector.tensor_tensor_scan(db[:, ::-1], dec, ek[:, ::-1], 0.0, ALU.mult, ALU.add)\
                            .then_inc(db_ok, 1)
                        wait(dve, ekv_ok, n + 1)
                        wait(dve, num_ok, n)
                        nc.vector.tensor_tensor_scan(nf, dec, ekv, 0.0, ALU.mult, ALU.add).then_inc(nf_ok, 1)
                        nc.vector.tensor_tensor_scan(nb[:, ::-1], dec, ekv[:, ::-1], 0.0, ALU.mult, ALU.add)\
                            .then_inc(nb_ok, 1)
                        wait(dve, er_raw, n + 1)
                        nc.vector.tensor_scalar(rbuf[p], rbuf[p], ER_CAP, None, ALU.min).then_inc(er_ok, 1)
                    if exists(n - 2):
                        wait(dve, lg_ok, n - 1)
                        if isinstance(n, int) and n == 2:
                            dve.wait_ge(lg_zero, 1)
                        wait(dve, lg_add, n - 2)
                        acc = lgacc[:, (n - 2) // NC, :]
                        nc.vector.tensor_tensor(acc, ps_lg[:, 0:TQ], acc, ALU.add).then_inc(lg_add, 1)
                    if exists(n - 1):
                        wait(dve, y_ok, n)
                        wait(dve, num_ok, n)
                        wait(dve, x0_out, (n - 1) * 16)
                        wait(dve, lg_ok, n - 1)
                        wait(dve, nat_ok, n - 1)
                        g = gain[:].rearrange("p b c -> p (b c)")[:, bass.ds(n - 1, 1)]
                        nc.vector.scalar_tensor_tensor(x0T, ps_num[1 - p][:, :], g, den[1 - p], ALU.mult, ALU.mult)\
                            .then_inc(x0_ok, 1)

                over_tiles(dve, body, 2)

            @block.gpsimd
            def _(pool):
                def body(n, p):
                    if exists(n):
                        wait(pool, delta_ok, n + 1)
                        nc.gpsimd.tensor_tensor(kbuf[p], delta[p], kbuf[p], ALU.mult).then_inc(dv_ok, 1)
                    if exists(n - 1):
                        wait(pool, l1_ok, n)
                        wait(pool, l2_ok, n)
                        nc.gpsimd.tensor_tensor(den[1 - p], den[1 - p], rbuf[1 - p], ALU.add).then_inc(s_ok, 1)
                    if exists(n):
                        wait(pool, df_ok, n + 1)
                        wait(pool, db_ok, n + 1)
                        nc.gpsimd.tensor_tensor(den[p], den[p], db, ALU.add).then_inc(sum1_ok, 1)
                        wait(pool, sum1_ok, n + 1)
                        nc.gpsimd.tensor_tensor(den[p], den[p], delta[p], ALU.add).then_inc(den_ok, 1)

                over_tiles(pool, body, 1)

            @block.tensor
            def _(pe):
                pe.wait_ge(c_id, 8)

                def body(n, p):
                    if exists(n - 2):
                        wait(pe, sq_ok, n - 1)
                        wait(pe, cws_ok, n - 1)
                        wait(pe, lg_add, n - 2)
                        for k, (w, v) in enumerate(((cws[:, p, :], x0T), (sumsq_w[:], sq))):
                            for q in range(Q):
                                last = nc.tensor.matmul(ps_lg[32 * q:32 * q + 32, 0:TQ], w,
                                                        v[:, q * TQ:(q + 1) * TQ], start=(k == 0), stop=(k == 1))
                        last.then_inc(lg_ok, 1)
                    if exists(n):
                        wait(pe, x0_ok, n - 1)
                        for k, (v, have, used) in enumerate(((kbuf[p], dv_ok, dv_used), (nf, nf_ok, None),
                                                             (nb, nb_ok, num_ok))):
                            wait(pe, have, n + 1)
                            for h in range(2):
                                cols = slice(512 * h, 512 * h + 512)
                                last = nc.tensor.matmul(ps_num[p][:, cols], ident[:], v[:, cols], start=(k == 0),
                                                        stop=(k == 2), skip_group_check=True)
                            if used:
                                last.then_inc(used, 1)
                    if exists(n - 1):
                        wait(pe, x0_ok, n)
                        wait(pe, nat_ev, n - 1)
                        for tc in range(NC):
                            last = nc.tensor.transpose(ps_nat[:, tc * P:(tc + 1) * P], x0T[:, tc * P:(tc + 1) * P],
                                                       ident[:])
                        last.then_inc(nat_ok, 1)

                over_tiles(pe, body, 2)

        CH = C // 2
        ring = [cut(at, 4096).rearrange("p (a c) -> p a c", a=4) for at in (0, 4096, 10240)]
        lgT, repl, ew = cut(10240, 1032), cut(11272, 1032), cut(12304, T)
        WTz = cut(8192, 1024).rearrange("p (t b s) -> p t b s", t=NC, b=B)
        Xb = cut(9216, C)
        XbT = cut(14336, NC * BS).rearrange("p (c s) -> p c s", c=NC)
        wbb, tsum = cut(14848, CH), cut(15360, CH)
        nat = [cut(14336, CH), cut(14848, CH)]
        kkz = cut(8192, 1024).rearrange("p (h b s) -> p h b s", h=HP, b=B)
        vvz = cut(9216, 1024).rearrange("p (h b s) -> p h b s", h=HP, b=B)
        stageA = [cut(10240 + 1024 * i, 1024) for i in range(4)]
        stageB = [cut(14336 + 1024 * i, 1024) for i in (0, 1)]
        Amat = cut(0, 4096).rearrange("p (i h x) -> p i h x", i=2, h=HP)
        Bmat = cut(10240, 4096).rearrange("p (i k x) -> p i k x", i=2, k=2)
        sbias = sb("sbias", [1, 2, HS])
        ab_in = [sem("AB_in_0"), sem("AB_in_1")]
        lognat = cut(16384, NC * BS).rearrange("p (t x) -> p t x", t=NC)
        wsT = cut(16384, NC * BS).rearrange("p (c x) -> p c x", c=NC)
        ws, npb = cut(16896, CH), cut(17920, C)
        brows = cut(17408, CH)
        sbrow, obrow = [brows[0:1, :], brows[32:33, :]], [brows[64:65, :], brows[96:97, :]]

        head_sems, tail_sems = {}, {}

        def stage_sem(held, name):
            if name not in held:
                held[name] = sem(name)
            return held[name]

        def load_batch(sp, t, b, part):
            i = b % 2
            if b < 2:
                h0, h1 = 2 * part, 2 * part + 2
            else:
                h0, h1 = 4 * part, 4 * part + 4
            if h0 < HP:
                sp.dma_start(Amat[:, i, h0:h1, :], A_d[b, h0:h1, :, :].rearrange("h p x -> p h x"))\
                    .then_inc(ab_in[t], 16)
            else:
                sp.dma_start(Bmat[:, i, part - 2, :], Bm_d[b, part - 2, :, :]).then_inc(ab_in[t], 16)
            if part == 3:
                sp.dma_start(sbias[:, i, :].rearrange("o (h r) -> o h r", h=HP),
                             sb_d[:, b:b + 1, :].rearrange("h o r -> o h r")).then_inc(ab_in[t], 16)

        def head(t):
            def hsem(name):
                return stage_sem(head_sems, f"head_{name}")

            c_in, st_s = hsem("rows_in"), hsem("bias_out")
            w_in = [hsem(f"weights_in_{i}") for i in range(3)]
            st_a = [hsem(f"A_out_{i}") for i in range(4)]
            st_b = [hsem("B_out_even"), hsem("B_out_odd")]
            if t == 0:
                lgt_ps, nat_rstd, nat_ln, lognat_ok = (
                    hsem(x) for x in ("lgt_ps", "nat_rstd", "nat_ln", "lognat_ok"))
            lgT_ps, lgT_ok, dtop, sel_ok, repl_ok = (hsem(x) for x in ("lgT_ps", "lgT_ok", "top", "sel", "repl"))
            e4_ok, e_ok, mask_ok, w_ok, wt_ps = (hsem(x) for x in ("e4", "e", "mask", "W", "WT_ps"))
            wtz0, wtz_ok, xb_ps, xb_a, xb_d = (hsem(x) for x in ("WTz0", "WTz", "Xb_ps", "Xb_act", "Xb_dve"))
            xbt_ps, xbt_ok, wr_ps, t1_ok, t2_ok = (hsem(x) for x in ("XbT_ps", "XbT", "write_ps", "t1", "t2"))
            ssq_ok, ln_ok, rs_ok, ws_ok, wst_ps = (hsem(x) for x in ("ssq", "ln", "rstd", "ws", "wsT_ps"))
            wsT_ok, kk_ps, kz, kk_ok, vv_ps, vv_ok = (hsem(x) for x in ("wsT", "kk_ps", "kkz0", "kk", "vv_ps", "vv"))
            ss_ps, kn_ok, vn_ok, kt_ps, vt_ps = (hsem(x) for x in ("ssq_ps", "kk_nat", "vv_nat", "kkT_ps", "vvT_ps"))
            prod_ps, ev_a, ev_d, sb_ps, sb_ok = (hsem(x) for x in ("prod_ps", "ev_act", "ev_dve", "sb_ps", "sb"))
            psA, psB, psX, ps3 = banks[0], banks[1], banks[3], banks[2]
            psC, psK = ps3[:, 0:512], ps3[:, 512:1024]
            psW, psT = psB[:, 0:512], psB[:, 512:1024]
            prod = [banks[0], banks[3]]

            with nc.Block() as block:
                @block.sync
                def _(sp):
                    def piece(slot, w, i):
                        sp.dma_start(ring[slot], w[:, 4 * i:4 * i + 4, :]).then_inc(w_in[slot], 16)

                    piece(0, wr_T, 0)
                    piece(1, wr_T, 1)
                    if t == 0:
                        sp.wait_ge(lgt_ps, 1)
                        for h in range(2):
                            half = slice(CH * h, CH * h + CH)
                            sp.dma_start(obrow[h], wo_b[half].rearrange("(o c) -> o c", o=1)).then_inc(c_in, 16)
                            sp.dma_start(ws[64 * h:64 * h + 64, :], work_t[:, half]).then_inc(c_in, 16)
                        sp.dma_start(npb, npost.rearrange("(o c) -> o c", o=1).broadcast_to([P, C])).then_inc(c_in, 16)
                    for h in range(2):
                        sp.dma_start(wbb[64 * h:64 * h + 64, :], wr_b[CH * h:CH * h + CH]
                                     .rearrange("(o c) -> o c", o=1).broadcast_to([BS, CH])).then_inc(c_in, 16)
                    for slot, w, i, free, count in ((2, wk_T, 0, wt_ps, 1), (0, wk_T, 1, wr_ps, 1),
                                                    (1, wv_T, 0, wr_ps, 2), (2, wv_T, 1, kk_ps, 1),
                                                    (0, wq, 0, kk_ps, 2), (1, wq, 1, vv_ps, 1)):
                        sp.wait_ge(free, count)
                        piece(slot, w, i)
                    sp.wait_ge(sb_ok, 2)
                    for h in range(2):
                        sp.dma_start(sb_d[4 * h:4 * h + 4, :, :].rearrange("(o h) b s -> o (h b s)", o=1), sbrow[h])\
                            .then_inc(st_s, 16)
                    for i in range(HP):
                        sp.wait_ge(ev_d if i % 2 else ev_a, i // 2 + 1)
                        sp.dma_start(A_d[:, i, :, :].rearrange("b p x -> p b x"),
                                     stageA[i % 4].rearrange("p (b x) -> p b x", b=B)).then_inc(st_a[i % 4], 16)
                        if i == 3:
                            piece(0, wo_T, 0)
                    piece(1, wo_T, 1)
                    for i in range(4):
                        sp.wait_ge(st_a[i], 16 * 2)
                    for i in range(HP, 2 * HP):
                        k, r32 = (i - HP) // 4, (i - HP) % 4 * 32
                        src, done = stageB[i % 2], st_b[i % 2]
                        sp.wait_ge(ev_d if i % 2 else ev_a, i // 2 + 1)
                        for b in range(2):
                            sp.dma_start(Bmat[r32:r32 + 32, b, k, :], src[32 * b:32 * b + 32, :]).then_inc(done, 16)
                        for b in range(2, B):
                            sp.dma_start(Bm_d[b, k, r32:r32 + 32, :], src[32 * b:32 * b + 32, :]).then_inc(done, 16)
                        if i == HP + 3:
                            sp.wait_ge(st_s, 32)
                            for part in range(4):
                                load_batch(sp, t, 0, part)
                    sp.wait_ge(st_b[0], 16 * 4 * B)
                    sp.wait_ge(st_b[1], 16 * 4 * B)
                    sp.wait_ge(ab_in[t], 80)

                @block.tensor
                def _(pe):
                    if t == 0:
                        for i in range(2 * B):
                            last = nc.tensor.transpose(psA[:, i * P:(i + 1) * P],
                                                       lgacc[:, i // 2, (i % 2) * P:(i % 2 + 1) * P], ident[:])
                        last.then_inc(lgt_ps, 1)
                        pe.wait_ge(lognat_ok, B)
                    for c in range(NC):
                        last = nc.tensor.transpose(psB[0:BS, c * P:(c + 1) * P], lognat[:, c, :], ident[:])
                    last.then_inc(lgT_ps, 1)
                    pe.wait_ge(w_ok, 1)
                    for c in range(NC):
                        last = nc.tensor.transpose(psC[:, c * BS:(c + 1) * BS], ew[0:BS, c * P:(c + 1) * P],
                                                   ident[0:BS, 0:BS])
                    last.then_inc(wt_ps, 1)
                    pe.wait_ge(wtz_ok, 1)
                    for c in range(NC):
                        for h in range(2):
                            for b in range(B):
                                last = nc.tensor.matmul(
                                    psX[32 * b:32 * b + 32, 512 * h:512 * h + 512], WTz[:, c, b, :],
                                    xres[:, b * NC + 4 * h:b * NC + 4 * h + 4, c, :],
                                    start=(c == 0), stop=(c == NC - 1), skip_group_check=True)
                    last.then_inc(xb_ps, 1)
                    pe.wait_ge(xb_a, 1)
                    pe.wait_ge(xb_d, 1)
                    for c in range(NC):
                        last = nc.tensor.transpose(psA[:, c * P:(c + 1) * P], Xb[:, c * P:(c + 1) * P], ident[:])
                    last.then_inc(xbt_ps, 1)
                    pe.wait_ge(xbt_ok, 1)

                    def project(ps, xT, i, slot, done):
                        for c in range(4 * i, 4 * i + 4):
                            for q in range(Q):
                                last = nc.tensor.matmul(
                                    ps[32 * q:32 * q + 32, :], xT[:, c, 32 * (q % 2):32 * (q % 2) + 32],
                                    ring[slot][:, c % 4, CH * (q // 2):CH * (q // 2) + CH],
                                    start=(c == 0), stop=(c == NC - 1), skip_group_check=True)
                        last.then_inc(done, 1)

                    def unfold(ps, src, done):
                        for j in range(4):
                            last = nc.tensor.transpose(ps[:, j * P:(j + 1) * P], src[:, j * P:(j + 1) * P], ident[:])
                        last.then_inc(done, 1)

                    for i in range(2):
                        pe.wait_ge(w_in[i], 16)
                        project(psW, XbT, i, i, wr_ps)
                    pe.wait_ge(ssq_ok, 1)
                    for h in range(2):
                        for k in range(2):
                            last = nc.tensor.matmul(psT[64 * h:64 * h + 64, 0:1], ident[:, 64 * k:64 * k + 64],
                                                    hstat[:, 0:1], start=(k == 0), stop=(k == 1),
                                                    skip_group_check=True)
                    last.then_inc(ss_ps, 1)
                    pe.wait_ge(ws_ok, 2)
                    unfold(psC, ws, wst_ps)
                    pe.wait_ge(wsT_ok, 1)
                    for i, slot, loads in ((0, 2, 1), (1, 0, 2)):
                        pe.wait_ge(w_in[slot], 16 * loads)
                        project(psK, wsT, i, slot, kk_ps)
                    for i, slot in ((0, 1), (1, 2)):
                        pe.wait_ge(w_in[slot], 16 * 2)
                        project(psC, wsT, i, slot, vv_ps)
                        if i == 0:
                            pe.wait_ge(kn_ok, 1)
                            unfold(psT, nat[0], kt_ps)
                    pe.wait_ge(kk_ok, 4)
                    for hp in range(HP):
                        r0 = 32 * (hp // 4)
                        last = nc.tensor.matmul(psK[r0:r0 + 1, hp % 4 * P:(hp % 4 + 1) * P], bqc[:, hp:hp + 1],
                                                kkz[:, hp, :, :], start=True, stop=True)
                    last.then_inc(sb_ps, 1)
                    pe.wait_ge(vn_ok, 1)
                    unfold(psW, nat[1], vt_ps)
                    for i in range(2 * HP):
                        hp, slot = i % HP, i % HP // 4
                        ps = prod[i % 2]
                        wait(pe, ev_d if i % 2 else ev_a, i // 2)
                        if i % 4 == 0:
                            pe.wait_ge(w_in[slot], 16 * (3 + i // HP))
                        if i < HP:
                            for c in range(NC):
                                last = nc.tensor.matmul(ps[:, c * P:(c + 1) * P],
                                                        ring[slot][:, hp % 4, c * P:(c + 1) * P], kkz[:, hp, :, :],
                                                        start=True, stop=True)
                        else:
                            pe.wait_ge(vv_ok, 4)
                            for h in range(2):
                                cols = slice(512 * h, 512 * h + 512)
                                last = nc.tensor.matmul(ps[:, cols], vvz[:, hp, :, :], ring[slot][:, hp % 4, cols],
                                                        start=True, stop=(hp > 0))
                                if hp == 0:
                                    last = nc.tensor.matmul(ps[:, cols], head0_row[h], obrow[h],
                                                            start=False, stop=True)
                        last.then_inc(prod_ps, 1)

                def copy_product(eng, copy, i):
                    eng.wait_ge(prod_ps, i + 1)
                    done = ev_d if i % 2 else ev_a
                    if i < HP:
                        wait(eng, st_a[i % 4], 16 * (i // 4))
                        copy(stageA[i % 4].rearrange("p (b c r) -> p b c r", b=B, c=NC),
                             prod[i % 2][:, :].rearrange("p (c b r) -> p b c r", c=NC, b=B)).then_inc(done, 1)
                    else:
                        wait(eng, st_b[i % 2], 16 * B * ((i - HP) // 2))
                        copy(stageB[i % 2], prod[i % 2][:, :]).then_inc(done, 1)

                @block.gpsimd
                def _(pool):
                    for s in cond_sems if t == 0 else tail_sems.values():
                        pool.sem_clear(s)

                @block.scalar
                def _(act):
                    nc.scalar.preload_act_table_set("natural_log_exp_and_others")
                    if t == 0:
                        act.wait_ge(lgt_ps, 1)
                        ss = psA[:, :].rearrange("p (g q r) -> p g q r", g=2 * B, q=Q)[:, :, :, S]
                        sm = small[:].rearrange("p (g q) -> p g q", g=2 * B)
                        nc.scalar.activation(sm, ss, ACT.Ln, bias=tiny[:, 2:3], scale=1.0 / C).then_inc(nat_ln, 1)
                        act.wait_ge(nat_ln, 1)
                        nc.scalar.activation(small[:], small[:], ACT.Exp, scale=-0.5).then_inc(nat_rstd, 1)
                    act.wait_ge(lgT_ps, 1)
                    nc.scalar.activation(lgT[0:BS, 0:T], psB[0:BS, :], ACT.Identity, bias=cbcol[:]).then_inc(lgT_ok, 1)
                    act.wait_ge(sel_ok, 2)
                    nc.scalar.activation(top8[:, 16:20], top8[:, 0:4], ACT.Exp, bias=top8[:, 20:21],
                                         accum_out=top8[:, 21:22]).then_inc(e4_ok, 1)
                    nc.scalar.activation(ew[0:BS, :], lgT[0:BS, 0:T], ACT.Exp, bias=top8[:, 20:21]).then_inc(e_ok, 1)
                    act.wait_ge(xb_ps, 1)
                    nc.scalar.activation(Xb[:, 0:512], psX[:, 0:512], ACT.Copy).then_inc(xb_a, 1)
                    act.wait_ge(t2_ok, 1)
                    nc.scalar.activation(nat[0], tsum, ACT.Square, accum_out=hstat[:, 0:1]).then_inc(ssq_ok, 1)
                    act.wait_ge(ss_ps, 1)
                    nc.scalar.activation(hstat[:, 1:2], psT[:, 0:1], ACT.Ln, bias=tiny[:, 2:3], scale=1.0 / C)\
                        .then_inc(ln_ok, 1)
                    act.wait_ge(ln_ok, 1)
                    nc.scalar.activation(hstat[:, 2:3], hstat[:, 1:2], ACT.Exp, scale=-0.5).then_inc(rs_ok, 1)
                    act.wait_ge(kk_ps, 2)
                    nc.scalar.activation(nat[0], psK, ACT.Copy).then_inc(kn_ok, 1)
                    act.wait_ge(vv_ps, 2)
                    nc.scalar.activation(nat[1], psC, ACT.Copy).then_inc(vn_ok, 1)
                    for i in range(0, 16, 2):
                        copy_product(act, lambda o, x: nc.scalar.activation(o, x, ACT.Copy), i)

                @block.vector
                def _(dve):
                    nc.vector.memset(WTz, 0.0).then_inc(wtz0, 1)
                    nc.vector.memset(lgT[0:BS, T:T + 4], BIG).then_inc(wtz0, 1)
                    if t == 0:
                        dve.wait_ge(nat_rstd, 1)
                        for b in range(B):
                            src = psA[:, b * 256:(b + 1) * 256].rearrange("p (h q r) -> p h q r", h=2, q=Q)
                            rst = small[:, b * 8:(b + 1) * 8].rearrange("p (h q o) -> p h q o", h=2, o=1)
                            dst = lognat[:, :, b * S:(b + 1) * S].rearrange("p (q h) s -> p h q s", h=2)
                            nc.vector.tensor_tensor(dst, src[:, :, :, 0:S], rst.broadcast_to([P, 2, Q, S]),
                                                    ALU.mult).then_inc(lognat_ok, 1)
                    dve.wait_ge(lgT_ok, 1)
                    nc.vector.max(top8[:, 0:8], lgT[0:BS, 0:T]).then_inc(dtop, 1)
                    dve.wait_ge(dtop, 1)
                    nc.vector.tensor_copy(top8[:, 8:12], top8[:, 0:4]).then_inc(sel_ok, 1)
                    nc.vector.tensor_scalar(top8[:, 20:21], top8[:, 0:1], -1.0, None, ALU.mult).then_inc(sel_ok, 1)
                    dve.wait_ge(sel_ok, 1)
                    dve.wait_ge(wtz0, 2)
                    nc.vector.match_replace(repl[0:BS, 0:T + 4], top8[:, 8:16], lgT[0:BS, 0:T + 4], -BIG)\
                        .then_inc(repl_ok, 1)
                    dve.wait_ge(repl_ok, 1)
                    nc.vector.tensor_tensor(repl[0:BS, 0:T], repl[0:BS, 0:T], lgT[0:BS, 0:T], ALU.not_equal)\
                        .then_inc(mask_ok, 1)
                    dve.wait_ge(e4_ok, 1)
                    nc.vector.reciprocal(top8[:, 22:23], top8[:, 21:22]).then_inc(mask_ok, 1)
                    dve.wait_ge(mask_ok, 2)
                    dve.wait_ge(e_ok, 1)
                    nc.vector.scalar_tensor_tensor(ew[0:BS, :], repl[0:BS, 0:T], top8[:, 22:23], ew[0:BS, :],
                                                   ALU.mult, ALU.mult).then_inc(w_ok, 1)
                    dve.wait_ge(wt_ps, 1)
                    nc.vector.tensor_copy(WTz[:, :, :, 0:S], psC.rearrange("p (t b s) -> p t b s", t=NC, b=B))\
                        .then_inc(wtz_ok, 1)
                    dve.wait_ge(c_in, 16 * (7 if t == 0 else 2))
                    nc.vector.tensor_tensor(wbb, wbb, ws, ALU.add).then_inc(t1_ok, 1)
                    dve.wait_ge(xb_ps, 1)
                    nc.vector.tensor_copy(Xb[:, 512:1024], psX[:, 512:1024]).then_inc(xb_d, 1)
                    dve.wait_ge(xbt_ps, 1)
                    nc.vector.tensor_copy(XbT.rearrange("p c (b s) -> p c b s", b=B),
                                          psA[:, :].rearrange("p (c b r) -> p c b r", c=NC, b=B)[:, :, :, 0:S])\
                        .then_inc(xbt_ok, 1)
                    nc.vector.memset(cut(8192, 2048), 0.0).then_inc(kz, 1)
                    dve.wait_ge(wr_ps, 2)
                    dve.wait_ge(t1_ok, 1)
                    nc.vector.tensor_tensor(tsum, psW, wbb, ALU.add).then_inc(t2_ok, 1)
                    dve.wait_ge(rs_ok, 1)
                    for h in range(2):
                        rows = slice(64 * h, 64 * h + 64)
                        nc.vector.scalar_tensor_tensor(ws[rows, :], tsum[rows, :], hstat[rows, 2:3],
                                                       npb[rows, CH * h:CH * h + CH], ALU.mult, ALU.mult)\
                            .then_inc(ws_ok, 1)
                    dve.wait_ge(wst_ps, 1)
                    nc.vector.tensor_copy(wsT.rearrange("p (h j) x -> p j h x", h=2),
                                          psC.rearrange("p (j h x) -> p j h x", j=4, h=2)).then_inc(wsT_ok, 1)
                    dve.wait_ge(kz, 1)
                    for ps, z, bias, have, done in ((psT, kkz, bkc, kt_ps, kk_ok), (psW, vvz, bvc, vt_ps, vv_ok)):
                        dve.wait_ge(have, 1)
                        for h in range(2):
                            for e in range(2):
                                rows = slice(64 * e, 64 * e + 64)
                                nc.vector.tensor_tensor(
                                    z[rows, 4 * h:4 * h + 4, :, S * e:S * e + S],
                                    ps[rows, :].rearrange("p (j g b s) -> p j g b s", j=4, g=2, b=B)[:, :, h, :, :],
                                    bias[rows, 4 * h:4 * h + 4].rearrange("p (h o i) -> p h o i", o=1, i=1)
                                    .broadcast_to([64, 4, B, S]), ALU.add).then_inc(done, 1)
                        if z is kkz:
                            dve.wait_ge(sb_ps, 1)
                            for h in range(2):
                                nc.vector.tensor_copy(sbrow[h], psK[32 * h:32 * h + 1, :]).then_inc(sb_ok, 1)
                    for i in range(1, 16, 2):
                        copy_product(dve, nc.vector.tensor_copy, i)

        xTb = [cut(4096 + 1024 * i, 1024).rearrange("p (c t) -> p c t", c=NC) for i in (0, 1)]
        x1s = [cut(6144 + 1024 * i, 1024) for i in (0, 1)]
        sc = [cut(8192 + 256 * i, 256) for i in (0, 1)]
        att, attT = cut(8704, 256), cut(8960, 256)
        y = cut(9216, C)
        x1T = cut(14336, C)
        xo = [cut(14336, C), cut(15360, C)]
        junks = [cut(15488, 512).bitcast(bf16), cut(16384, 512).bitcast(bf16)]
        lp = cut(15360, P)
        stat = sb("stat", [P, 8])
        mx, den16 = sb("mx", [P, H]), sb("den16", [P, H])

        def tail(t):
            first = t == 0
            junk = junks[t]

            def tsem(name):
                return stage_sem(tail_sems, f"tail_{name}")

            xT_in, x1_out, xo_in = (
                [tsem(f"{v}_even"), tsem(f"{v}_odd")] for v in ("xT_in", "x1_out", "xo_in"))
            sc_ps, mx_ok, sub_ok, e_ok, sum_ok, rc_ok, att_ok = (
                tsem(v) for v in ("scores_ps", "max", "sub", "exp", "sum", "rcp", "att"))
            at_ps, at_ev, o_ps, y_ok, ssq_ok, ln_ok, rs_ok, x1_ok = (
                tsem(v) for v in ("attT_ps", "attT", "out_ps", "y", "ssq", "ln", "rstd", "x1"))
            if first:
                x1T_out, xt_ps, xt_ev, ssq2_ok, ln2_ok, rs2_ok, l_ps, lp_ok, l2_ps, l_ok = (
                    tsem(v) for v in ("x1T_out", "x1T_ps", "x1T", "ssq2", "ln2", "rstd2", "l_ps", "lp",
                                      "l2_ps", "logits"))
            else:
                fin = tsem("final")
            ps_s = [banks[0][:, 0:256], banks[0][:, 512:768]]
            ps_at, ps_l = banks[1][:, 0:256], banks[1][:, 512:640]
            ps_l2 = banks[1][:, 640:656]
            ps_o, ps_x = banks[2], banks[3]

            with nc.Block() as block:
                @block.sync
                def _(sp):
                    def load_x(b, tc, m, p):
                        wait(sp, sc_ps, m - 1)
                        if first:
                            src = x0T_d[b * NC:(b + 1) * NC, :, bass.ds(tc * P, P)].rearrange("c p t -> p c t")
                        else:
                            src = x1T_d[m, :, :].rearrange("p (c t) -> p c t", c=NC)
                        sp.dma_start(xTb[p], src).then_inc(xT_in[p], 16)

                    def store(m, p):
                        if first:
                            wait(sp, x1_ok, m + 1)
                            sp.dma_start(xres[:, bass.ds(m // NC * NC, NC), m % NC, :],
                                         x1s[p].rearrange("p (c x) -> p c x", c=NC)).then_inc(x1_out[p], 16)
                            wait(sp, xt_ev, m + 1)
                            sp.dma_start(x1T_d[m, :, :], x1T).then_inc(x1T_out, 16)
                        else:
                            wait(sp, fin, m + 1)
                            sp.dma_start(out[m, :, :], x1s[p]).then_inc(x1_out[p], 16)

                    def load_residual(m, p):
                        if not first:
                            wait(sp, fin, m - 1)
                            sp.dma_start(xo[p], x[m, :, :]).then_inc(xo_in[p], 16)

                    def step(b, tc, m, p):
                        load_x(b, tc, m, p)
                        if exists(m - 3):
                            store(m - 3, 1 - p)
                        if exists(m - 1):
                            load_residual(m - 1, 1 - p)

                    for b in range(B):
                        if b == 0:
                            for tc in range(4):
                                step(0, tc, tc, tc % 2)
                        else:
                            with sp.Fori(0, 2) as j:
                                for p in range(2):
                                    step(b, j * 2 + p, j * 2 + (b * NC + p), p)
                        for tc in range(4, NC):
                            if b + 1 < B:
                                if tc == 4:
                                    wait(sp, o_ps, NC * b)
                                    sp.wait_ge(ab_in[t], 80 * (b + 1))
                                load_batch(sp, t, b + 1, tc - 4)
                            step(b, tc, b * NC + tc, tc % 2)
                    for m in range(NT - 3, NT):
                        store(m, m % 2)
                        if m == NT - 3:
                            load_residual(NT - 1, 1)
                    for p in range(2):
                        sp.wait_ge(x1_out[p], 16 * NT // 2)
                    if first:
                        sp.wait_ge(x1T_out, 16 * NT)

                @block.tensor
                def _(pe):
                    def scores(m, p, part):
                        i = m // NC % 2
                        if part == 0:
                            wait(pe, ab_in[t], (m // NC + 1) * 80)
                            wait(pe, xT_in[p], (m // 2 + 1) * 16)
                            wait(pe, sub_ok, m - 1)
                            nc.tensor.matmul(ps_s[p], ones_row, sbias[:, i, :], start=True, stop=False)
                        for c in range(4 * part, 4 * part + 4):
                            last = nc.tensor.matmul(ps_s[p], xTb[p][:, c, :], Amat[:, i, :, c * 32:c * 32 + 32],
                                                    start=False, stop=(c == NC - 1))
                        if part == 1:
                            last.then_inc(sc_ps, 1)

                    def body(m, p):
                        if exists(m + 1):
                            scores(m + 1, 1 - p, 0)
                        if exists(m):
                            wait(pe, att_ok, m + 1)
                            wait(pe, at_ev, m)
                            for k in range(2):
                                last = nc.tensor.transpose(ps_at[:, k * P:(k + 1) * P], att[:, k * P:(k + 1) * P],
                                                           ident[:])
                            last.then_inc(at_ps, 1)
                        if exists(m + 1):
                            scores(m + 1, 1 - p, 1)
                        if exists(m):
                            i = m // NC % 2
                            wait(pe, at_ev, m + 1)
                            wait(pe, y_ok, m)
                            for k in range(2):
                                for h in range(2):
                                    cols = slice(512 * h, 512 * h + 512)
                                    last = nc.tensor.matmul(ps_o[:, cols], attT[:, k * P:(k + 1) * P],
                                                            Bmat[:, i, k, cols], start=(k == 0), stop=(k == 1),
                                                            skip_group_check=True)
                            last.then_inc(o_ps, 1)
                        if first and exists(m - 2):
                            wait(pe, xt_ev, m - 1)
                            wait(pe, l_ok, m - 2)
                            for c in range(NC):
                                q = c % Q
                                last = nc.tensor.matmul(ps_l[32 * q:32 * q + 32, :], cwz[:, c, :],
                                                        x1T[:, c * P:(c + 1) * P], start=(c < Q), stop=(c >= Q),
                                                        skip_group_check=True)
                            last.then_inc(l_ps, 1)
                        if first and exists(m - 1):
                            wait(pe, x1_ok, m)
                            for c in range(NC):
                                last = nc.tensor.transpose(ps_x[:, c * P:(c + 1) * P],
                                                           x1s[1 - p][:, c * P:(c + 1) * P], ident[:])
                            last.then_inc(xt_ps, 1)
                        if first and exists(m - 2):
                            wait(pe, lp_ok, m - 1)
                            nc.tensor.matmul(ps_l2, lp, fold[:], start=True, stop=True).then_inc(l2_ps, 1)

                    scores(0, 0, 0)
                    scores(0, 0, 1)
                    over_tiles(pe, body, 2 if first else 0)

                @block.vector
                def _(dve):
                    def submax(m, p):
                        s3 = ps_s[p].rearrange("p (h s) -> p h s", h=H)
                        wait(dve, sc_ps, m + 1)
                        nc.vector.tensor_reduce(mx[:], s3, AXX, ALU.max).then_inc(mx_ok, 1)
                        wait(dve, mx_ok, m + 1)
                        nc.vector.tensor_tensor(sc[p].rearrange("p (h s) -> p h s", h=H), s3,
                                                mx[:].rearrange("p (h o) -> p h o", o=1).broadcast_to([P, H, S]),
                                                ALU.subtract).then_inc(sub_ok, 1)

                    def body(m, p):
                        if first and exists(m - 3):
                            n = m - 3
                            wait(dve, l2_ps, m - 2)
                            wait(dve, rs2_ok, m - 2)
                            nc.vector.tensor_scalar(lognat[:, n % NC, bass.ds(n // NC * S, S)], ps_l2,
                                                    stat2[1 - p][:, 2:3],
                                                    None, ALU.mult).then_inc(l_ok, 1)
                        if exists(m):
                            e3 = sc[p].rearrange("p (h s) -> p h s", h=H)
                            wait(dve, e_ok, m + 1)
                            nc.vector.tensor_reduce(den16[:], e3, AXX, ALU.add).then_inc(sum_ok, 1)
                            wait(dve, sum_ok, m + 1)
                            nc.vector.reciprocal(den16[:], den16[:]).then_inc(rc_ok, 1)
                            wait(dve, rc_ok, m + 1)
                            wait(dve, at_ps, m)
                            nc.vector.tensor_tensor(att.rearrange("p (h s) -> p h s", h=H), e3,
                                                    den16[:].rearrange("p (h o) -> p h o", o=1)
                                                    .broadcast_to([P, H, S]), ALU.mult).then_inc(att_ok, 1)
                        if exists(m - 1):
                            n = m - 1
                            wait(dve, o_ps, m)
                            wait(dve, x1_ok, m - 1)
                            nc.vector.tensor_tensor(y.rearrange("p (c x) -> p c x", c=NC),
                                                    ps_o[:, :].rearrange("p (c x) -> p c x", c=NC),
                                                    xres[:, bass.ds(n // NC * NC, NC), n % NC, :],
                                                    ALU.add).then_inc(y_ok, 1)
                        if exists(m + 1):
                            submax(m + 1, 1 - p)
                        if exists(m - 1):
                            wait(dve, rs_ok, m)
                            wait(dve, x1_out[1 - p], (m - 1) // 2 * 16)
                            if first:
                                wait(dve, xt_ps, m - 2)
                                wait(dve, ssq2_ok, m - 2)
                            nc.vector.scalar_tensor_tensor(x1s[1 - p], y, stat[:, 2:3], npb, ALU.mult, ALU.mult)\
                                .then_inc(x1_ok, 1)

                    submax(0, 0)
                    over_tiles(dve, body, 3 if first else 1)

                @block.scalar
                def _(act):
                    nc.scalar.preload_act_table_set("natural_log_exp_and_others")

                    def expo(m, p):
                        wait(act, sub_ok, m + 1)
                        nc.scalar.activation(sc[p], sc[p], ACT.Exp, scale=SCALE).then_inc(e_ok, 1)

                    def body(m, p):
                        if exists(m - 1):
                            wait(act, y_ok, m)
                            nc.scalar.activation(junk, y, ACT.Square, accum_out=stat[:, 0:1]).then_inc(ssq_ok, 1)
                            wait(act, ssq_ok, m)
                            nc.scalar.activation(stat[:, 1:2], stat[:, 0:1], ACT.Ln, bias=tiny[:, 2:3],
                                                 scale=1.0 / C).then_inc(ln_ok, 1)
                            wait(act, ln_ok, m)
                            nc.scalar.activation(stat[:, 2:3], stat[:, 1:2], ACT.Exp, scale=-0.5).then_inc(rs_ok, 1)
                        if exists(m):
                            wait(act, at_ps, m + 1)
                            wait(act, o_ps, m)
                            nc.scalar.activation(attT, ps_at, ACT.Copy).then_inc(at_ev, 1)
                        if exists(m + 1):
                            expo(m + 1, 1 - p)
                        if first and exists(m - 2):
                            wait(act, l_ps, m - 1)
                            nc.scalar.activation(lp, ps_l, ACT.Copy).then_inc(lp_ok, 1)
                        if first and exists(m - 1):
                            q = stat2[1 - p]
                            wait(act, x1_ok, m)
                            wait(act, l_ok, m - 2)
                            nc.scalar.activation(junk, x1s[1 - p], ACT.Square, accum_out=q[:, 0:1])\
                                .then_inc(ssq2_ok, 1)
                            wait(act, ssq2_ok, m)
                            nc.scalar.activation(q[:, 1:2], q[:, 0:1], ACT.Ln, bias=tiny[:, 2:3],
                                                 scale=1.0 / C).then_inc(ln2_ok, 1)
                            wait(act, ln2_ok, m)
                            nc.scalar.activation(q[:, 2:3], q[:, 1:2], ACT.Exp, scale=-0.5).then_inc(rs2_ok, 1)
                            wait(act, xt_ps, m)
                            wait(act, l_ps, m - 1)
                            wait(act, x1T_out, (m - 1) * 16)
                            nc.scalar.activation(x1T, ps_x[:, :], ACT.Copy).then_inc(xt_ev, 1)

                    expo(0, 0)
                    over_tiles(act, body, 2 if first else 1)

                if first:
                    @block.gpsimd
                    def _(pool):
                        for s in head_sems.values():
                            pool.sem_clear(s)
                else:
                    @block.gpsimd
                    def _(pool):
                        def body(m, p):
                            wait(pool, x1_ok, m + 1)
                            wait(pool, xo_in[p], (m // 2 + 1) * 16)
                            nc.gpsimd.tensor_tensor(x1s[p], x1s[p], xo[p], ALU.add).then_inc(fin, 1)

                        over_tiles(pool, body, 0)

        stat2 = [sb("stat_even", [P, 4]), sb("stat_odd", [P, 4])]
        for t in range(2):
            head(t)
            if t == 0:
                cond_ctx.close()
            tail(t)


def kernel(**inputs):
    import numpy as np
    import concourse.bacc as bacc
    from concourse.bass_utils import run_bass_kernel_spmd

    i = {k: np.asarray(v) for k, v in inputs.items()}

    def cols(v, rep=1):
        return np.tile(v.reshape(-1, P).T, (1, rep))

    def chunked(w):
        return w.reshape(-1, P, w.shape[1]).transpose(1, 0, 2)

    ipw, ipb = i["L0_ffn_in_proj_w"], i["L0_ffn_in_proj_b"]
    arrays = {
        "xT": i["x"].transpose(0, 2, 1).reshape(NT, P, T),
        "kT": i["fside_BxSxS_0"].transpose(0, 2, 1).reshape(NT, P, T),
        "x_nat": i["x"].reshape(NT, P, C),
        "cond": i["cond_512"],
        "w_cols": cols(i["L0_cond_w"], B),
        "u_cols": cols(i["L0_cond_u"], B),
        "workspace": np.tile(i["L0_ffn_workspace"], (B, 1)),
        "cw_cols": chunked(i["L0_ffn_compete_w"].T).reshape(P, NC * S),
        "npre_cols": cols(i["L0_ffn_norm_pre_w"]),
        "cb_col": np.tile(i["L0_ffn_compete_b"], B).reshape(BS, 1),
        "wr_T": chunked(i["L0_ffn_write_w"].T),
        "wr_b": i["L0_ffn_write_b"],
        "wq": chunked(ipw[:C]),
        "wk_T": chunked(ipw[C:2 * C].T),
        "wv_T": chunked(ipw[2 * C:].T),
        "bq_cols": cols(ipb[:C]),
        "bk_cols": cols(ipb[C:2 * C]),
        "bv_cols": cols(ipb[2 * C:]),
        "wo_T": chunked(i["L0_ffn_out_proj_w"].T),
        "wo_b": i["L0_ffn_out_proj_b"],
        "npost": i["L0_ffn_norm_post_w"],
    }
    nc = bacc.Bacc("TRN2", target_bir_lowering=False, num_devices=1)
    fed, args = {}, []
    for name, a in arrays.items():
        a = np.ascontiguousarray(a)
        fed[f"in_{name}"] = a
        args.append(nc.dram_tensor(f"in_{name}", a.shape, mybir.dt.from_np(a.dtype), kind="ExternalInput").ap())
    args.append(nc.dram_tensor("out_0", [NT, P, C], fp32, kind="ExternalOutput").ap())
    build(nc, *args)
    r = run_bass_kernel_spmd(nc, [fed], core_ids=[0])
    return r.results[0]["out_0"].reshape(B, T, C)
```

```python
import concourse.bass as bass
from concourse import mybir
from contextlib import ExitStack

fp32 = mybir.dt.float32
bf16 = mybir.dt.bfloat16
ALU = mybir.AluOpType
ACT = mybir.ActivationFunctionType
AXX = mybir.AxisListType.X

P = 128
B, T, C = 4, 1024, 1024
TD = 256
S, K = 16, 4
H = C // 64
NC = C // P
NT = B * NC
BS = B * S
HS = H * S
HP = H // 2
Q = 4
TQ = T // Q
EXP_CAP = 10686474581524.463
ER_CAP = 2.0 ** 62
BIG = 3.0e38
SCALE = 0.125


def wait(eng, sem, count):
    if not (isinstance(count, int) and count <= 0):
        eng.wait_ge(sem, count)


def exists(n):
    return not isinstance(n, int) or 0 <= n < NT


def over_tiles(eng, body, lag):
    fill = 4
    for n in range(fill):
        body(n, n % 2)
    with eng.Fori(fill // 2, NT // 2 - 1) as j:
        for p in range(2):
            body(j * 2 + p, p)
    for n in range(NT - 2, NT + lag):
        body(n, n % 2)


def build(nc, xT, kT, x, cond, w_cols, u_cols, work_t, cw_cols, npre_cols, cb_col, wr_T, wr_b, wq, wk_T,
          wv_T, bq_cols, bk_cols, bv_cols, wo_T, wo_b, npost, out):
    with ExitStack() as ctx:
        def sb(name, shape, dt=fp32):
            return ctx.enter_context(nc.sbuf_tensor(name, shape, dt))

        def sem(name):
            return ctx.enter_context(nc.semaphore(name))

        x0T_d = nc.dram_tensor("x0T_scratch", [NT, P, T], fp32).ap()
        x1T_d = nc.dram_tensor("x1T_scratch", [NT, P, C], fp32).ap()
        A_d = nc.dram_tensor("A_scratch", [B, HP, P, NC * 32], fp32).ap()
        Bm_d = nc.dram_tensor("B_scratch", [B, 2, P, C], fp32).ap()
        sb_d = nc.dram_tensor("score_bias_scratch", [B, HP, 32], fp32).ap()

        xres = sb("xres", [P, NT, NC, P])
        ident = sb("ident", [P, P])
        cwz = sb("cwz", [P, NC, 32])
        cws = sb("cws", [P, 2, 32])
        sumsq_w = sb("sumsq_w", [P, 32])
        fold = sb("fold", [P, S])
        rows = sb("rows", [P, P])
        ones_row, head0_row = rows[0:1, :], [rows[64:65, :], rows[96:97, :]]
        tiny = sb("tiny", [P, 4])
        decay = sb("decay", [P, B, NC])
        gain = sb("gain", [P, B, NC])
        ucol = sb("ucol", [P, NT])
        wcol = sb("wcol", [P, NT])
        small = sb("small", [P, 32])
        cbcol = sb("cbcol", [BS, 1])
        bqc = sb("bqc", [P, HP])
        bkc = sb("bkc", [P, HP])
        bvc = sb("bvc", [P, HP])
        nprec = sb("nprec", [P, NC])
        top8 = sb("top8", [BS, 24])
        hstat = sb("hstat", [P, 4])
        work = sb("work", [P, 18944])

        def cut(at, n):
            return work[:, at:at + n]

        banks = [ctx.enter_context(nc.psum_tensor(f"bank{i}", [P, 2 * 512], fp32)) for i in range(4)]

        cin = sem("const_in")
        c_id = sem("const_ident")
        c_dve = sem("const_dve")
        c_act = sem("const_act")
        condb = cut(16384, B * TD)
        cwraw = cut(15360, NC * S)

        cond_sems = []
        cond_ctx = ExitStack()

        def csem(name):
            cond_sems.append(cond_ctx.enter_context(nc.semaphore(name)))
            return cond_sems[-1]

        k_in = [csem("k_in_even"), csem("k_in_odd")]
        r_in = [csem("r_in_even"), csem("r_in_odd")]
        kbuf = [cut(1024 * i, T) for i in (0, 1)]
        rbuf = [cut(1024 * i, T) for i in (2, 9)]

        with nc.Block() as block:
            @block.sync
            def _(sp):
                sp.dma_start(kbuf[0], kT[0, :, :]).then_inc(k_in[0], 16)
                sp.dma_start(condb.rearrange("p (b d) -> p b d", b=B),
                             cond.rearrange("(o b) d -> o b d", o=1).broadcast_to([P, B, TD])).then_inc(cin, 16)
                for dst, src in ((wcol[:], w_cols), (ucol[:], u_cols), (cwraw, cw_cols), (nprec[:], npre_cols),
                                 (cbcol[:], cb_col), (bqc[:], bq_cols), (bkc[:], bk_cols), (bvc[:], bv_cols)):
                    sp.dma_start(dst, src).then_inc(cin, 16)
                sp.dma_start(rbuf[0], xT[0, :, :]).then_inc(r_in[0], 16)
                sp.dma_start(kbuf[1], kT[1, :, :]).then_inc(k_in[1], 16)

            @block.gpsimd
            def _(pool):
                nc.gpsimd.memset(ident[:], 0.0).then_inc(c_id, 1)
                nc.gpsimd.memset(fold[:], 0.0).then_inc(c_id, 1)
                nc.gpsimd.memset(ones_row, 1.0).then_inc(c_id, 1)
                pool.wait_ge(c_id, 3)
                nc.gpsimd.affine_select(out=ident[:], in_=ident[:], compare_op=ALU.not_equal, fill=1.0, base=0,
                                        pattern=[[-1, P]], channel_multiplier=1).then_inc(c_id, 1)
                for q in range(Q):
                    nc.gpsimd.affine_select(out=fold[:], in_=fold[:], compare_op=ALU.not_equal, fill=1.0,
                                            base=-32 * q, pattern=[[-1, S]], channel_multiplier=1).then_inc(c_id, 1)
                    pool.wait_ge(c_id, 5 + q)

            @block.vector
            def _(dve):
                n = [0]

                def step(ins):
                    n[0] += 1
                    ins.then_inc(c_dve, 1)
                    dve.wait_ge(c_dve, n[0])

                step(nc.vector.memset(tiny[:, 0:1], -1e-8))
                step(nc.vector.memset(tiny[:, 1:2], 1e-8))
                step(nc.vector.memset(tiny[:, 2:4], 1e-6))
                step(nc.vector.memset(cwz[:], 0.0))
                step(nc.vector.memset(sumsq_w[:], 0.0))
                step(nc.vector.memset(sumsq_w[:, S:S + 1], 1.0))
                step(nc.vector.memset(head0_row[0], 0.0))
                step(nc.vector.memset(head0_row[0].rearrange("o (b r) -> o b r", b=B)[:, :, 0:S], 1.0))
                step(nc.vector.memset(top8[:, 8:16], BIG))
                dve.wait_ge(cin, 9 * 16)
                step(nc.vector.tensor_reduce(small[:, 0:4], condb.rearrange("p (b d) -> p b d", b=B), AXX, ALU.add))
                step(nc.vector.tensor_tensor(cwz[:, :, 0:S], cwraw.rearrange("p (c s) -> p c s", c=NC),
                                             nprec[:].rearrange("p (c o) -> p c o", o=1).broadcast_to([P, NC, S]),
                                             ALU.mult))
                dve.wait_ge(c_act, 3)
                step(nc.vector.tensor_scalar(small[:, 8:12], small[:, 4:8], 1.0, None, ALU.add))
                step(nc.vector.reciprocal(small[:, 12:16], small[:, 8:12]))
                step(nc.vector.tensor_scalar(small[:, 16:20], small[:, 12:16], 0.5, 0.5, ALU.mult, ALU.add))
                step(nc.vector.tensor_scalar(small[:, 20:24], small[:, 12:16], 0.2, 0.8, ALU.mult, ALU.add))
                half = small[:, 16:20].rearrange("p (b o) -> p b o", o=1).broadcast_to([P, B, NC])
                g4 = small[:, 20:24].rearrange("p (b o) -> p b o", o=1).broadcast_to([P, B, NC])
                step(nc.vector.tensor_tensor(decay[:], wcol[:].rearrange("p (b c) -> p b c", b=B), half, ALU.mult))
                step(nc.vector.tensor_copy(gain[:], g4))
                step(nc.vector.memset(head0_row[1], 0.0))
                step(nc.vector.memset(head0_row[1].rearrange("o (b r) -> o b r", b=B)[:, :, 0:S], 1.0))

            @block.scalar
            def _(act):
                nc.scalar.preload_act_table_set("natural_log_exp_and_others")
                act.wait_ge(cin, 9 * 16)
                nc.scalar.activation(wcol[:], wcol[:], ACT.Exp).then_inc(c_act, 1)
                act.wait_ge(c_act, 1)
                nc.scalar.activation(wcol[:], wcol[:], ACT.Exp, scale=-1.0).then_inc(c_act, 1)
                act.wait_ge(c_dve, 10)
                nc.scalar.activation(small[:, 4:8], small[:, 0:4], ACT.Exp, scale=-1.0).then_inc(c_act, 1)

        ekr = cut(3072, T)
        ek = cut(4096, T)
        ekv = cut(5120, T)
        eur = cut(6144, T)
        delta = [cut(1024 * i, T) for i in (7, 8)]
        nf = cut(10240, T)
        nb = cut(11264, T)
        den = [cut(1024 * i, T) for i in (12, 13)]
        db = cut(14336, T)
        x0T = cut(15360, T)
        sq = cut(16384, T)
        lgacc = cut(17408, B * TQ).rearrange("p (b t) -> p b t", b=B)
        ps_num = banks[0:2]
        ps_nat = banks[2]
        ps_lg = banks[3]

        x0_out = csem("x0_out")
        ek_raw, eu_raw, er_raw = csem("ek_raw"), csem("eu_raw"), csem("er_raw")
        ek_ok, er_ok, ekv_ok, delta_ok = csem("ek_ok"), csem("er_ok"), csem("ekv_ok"), csem("delta_ok")
        df_ok, db_ok, nf_ok, nb_ok = csem("df_ok"), csem("db_ok"), csem("nf_ok"), csem("nb_ok")
        dv_ok, sum1_ok, den_ok = csem("dv_ok"), csem("sum1_ok"), csem("den_ok")
        l1_ok, guard_ok, l2_ok, s_ok, y_ok = csem("l1_ok"), csem("guard_ok"), csem("l2_ok"), csem("s_ok"), csem("y_ok")
        num_ok, x0_ok, sq_ok, cws_ok = csem("num_ok"), csem("x0_ok"), csem("sq_ok"), csem("cws_ok")
        nat_ok, nat_ev, lg_ok, lg_add = csem("nat_ok"), csem("nat_ev"), csem("lg_ok"), csem("lg_add")
        dv_used, lg_zero = csem("dv_used"), csem("lg_zero")

        with nc.Block() as block:
            @block.sync
            def _(sp):
                def body(n, p):
                    if exists(n + 1) and not (isinstance(n, int) and n == 0):
                        wait(sp, dv_used, n)
                        sp.dma_start(kbuf[1 - p], kT[n + 1, :, :]).then_inc(k_in[1 - p], 16)
                    if exists(n) and not (isinstance(n, int) and n == 0):
                        wait(sp, s_ok, n - 1)
                        sp.dma_start(rbuf[p], xT[n, :, :]).then_inc(r_in[p], 16)
                    if exists(n - 2):
                        wait(sp, x0_ok, n - 1)
                        sp.dma_start(x0T_d[n - 2, :, :], x0T).then_inc(x0_out, 16)

                over_tiles(sp, body, 2)
                sp.wait_ge(x0_out, 16 * NT)

            @block.scalar
            def _(act):
                act.wait_ge(c_dve, 19)

                def exps(n, p):
                    wait(act, k_in[p], (n // 2 + 1) * 16)
                    wait(act, ek_ok, n)
                    nc.scalar.activation(ekr, kbuf[p], ACT.Exp).then_inc(ek_raw, 1)
                    wait(act, delta_ok, n)
                    nc.scalar.activation(eur, kbuf[p], ACT.Exp, bias=ucol[:, bass.ds(n, 1)]).then_inc(eu_raw, 1)

                nc.scalar.preload_act_table_set("natural_log_exp_and_others")
                exps(0, 0)

                def body(n, p):
                    if exists(n - 1):
                        wait(act, er_ok, n)
                        nc.scalar.activation(rbuf[1 - p], rbuf[1 - p], ACT.Ln, bias=1.0).then_inc(l1_ok, 1)
                        wait(act, den_ok, n)
                        d = den[1 - p]
                        nc.scalar.activation(d, d, ACT.Relu, bias=tiny[:, 0:1]).then_inc(guard_ok, 1)
                        wait(act, guard_ok, n)
                        nc.scalar.activation(d, d, ACT.Ln, bias=tiny[:, 1:2]).then_inc(l2_ok, 1)
                    if exists(n):
                        wait(act, r_in[p], (n // 2 + 1) * 16)
                        nc.scalar.activation(rbuf[p], rbuf[p], ACT.Exp, scale=-1.0).then_inc(er_raw, 1)
                    if exists(n - 2):
                        wait(act, x0_ok, n - 1)
                        wait(act, lg_ok, n - 2)
                        nc.scalar.activation(sq, x0T, ACT.Square).then_inc(sq_ok, 1)
                        nc.scalar.activation(cws[:, p, :], cwz[:, (n - 2) % NC, :], ACT.Copy).then_inc(cws_ok, 1)
                    if exists(n + 1):
                        exps(n + 1, 1 - p)
                    if exists(n - 1):
                        wait(act, s_ok, n)
                        nc.scalar.activation(den[1 - p], den[1 - p], ACT.Exp, scale=-1.0).then_inc(y_ok, 1)
                    if exists(n - 2):
                        wait(act, nat_ok, n - 1)
                        nc.scalar.activation(xres[:, n - 2, :, :].rearrange("p a c -> p (a c)"), ps_nat[:, :],
                                             ACT.Copy).then_inc(nat_ev, 1)

                over_tiles(act, body, 2)

            @block.vector
            def _(dve):
                nc.vector.memset(lgacc, 0.0).then_inc(lg_zero, 1)

                def body(n, p):
                    if exists(n):
                        wait(dve, ek_raw, n + 1)
                        wait(dve, df_ok, n)
                        nc.vector.tensor_scalar(ek, ekr, EXP_CAP, None, ALU.min).then_inc(ek_ok, 1)
                    if exists(n - 3):
                        wait(dve, lg_ok, n - 2)
                        if isinstance(n, int) and n == 3:
                            dve.wait_ge(lg_zero, 1)
                        wait(dve, lg_add, n - 3)
                        acc = lgacc[:, (n - 3) // NC, :]
                        nc.vector.tensor_tensor(acc, ps_lg[:, 0:TQ], acc, ALU.add).then_inc(lg_add, 1)
                    if exists(n):
                        wait(dve, ek_ok, n + 1)
                        wait(dve, nb_ok, n)
                        nc.vector.tensor_tensor(ekv, ek, kbuf[p], ALU.mult).then_inc(ekv_ok, 1)
                        wait(dve, eu_raw, n + 1)
                        wait(dve, den_ok, n - 1)
                        nc.vector.scalar_tensor_tensor(delta[p], eur, EXP_CAP, ek, ALU.min, ALU.subtract)\
                            .then_inc(delta_ok, 1)
                    if exists(n - 2):
                        wait(dve, y_ok, n - 1)
                        wait(dve, num_ok, n - 1)
                        wait(dve, x0_out, (n - 2) * 16)
                        wait(dve, lg_ok, n - 2)
                        wait(dve, nat_ok, n - 2)
                        g = gain[:].rearrange("p b c -> p (b c)")[:, bass.ds(n - 2, 1)]
                        nc.vector.scalar_tensor_tensor(x0T, ps_num[p][:, :], g, den[p], ALU.mult, ALU.mult)\
                            .then_inc(x0_ok, 1)
                    if exists(n):
                        dec = decay[:].rearrange("p b c -> p (b c)")[:, bass.ds(n, 1)].broadcast_to([P, T])
                        wait(dve, sum1_ok, n)
                        nc.vector.tensor_tensor_scan(db[:, ::-1], dec, ek[:, ::-1], 0.0, ALU.mult, ALU.add)\
                            .then_inc(db_ok, 1)
                        wait(dve, x0_ok, n - 1)
                        nc.vector.tensor_tensor_scan(den[p], dec, ek, 0.0, ALU.mult, ALU.add).then_inc(df_ok, 1)
                        wait(dve, ekv_ok, n + 1)
                        wait(dve, num_ok, n)
                        nc.vector.tensor_tensor_scan(nf, dec, ekv, 0.0, ALU.mult, ALU.add).then_inc(nf_ok, 1)
                        nc.vector.tensor_tensor_scan(nb[:, ::-1], dec, ekv[:, ::-1], 0.0, ALU.mult, ALU.add)\
                            .then_inc(nb_ok, 1)
                        wait(dve, er_raw, n + 1)
                        nc.vector.tensor_scalar(rbuf[p], rbuf[p], ER_CAP, None, ALU.min).then_inc(er_ok, 1)

                over_tiles(dve, body, 3)

            @block.gpsimd
            def _(pool):
                def body(n, p):
                    if exists(n):
                        wait(pool, delta_ok, n + 1)
                        nc.gpsimd.tensor_tensor(kbuf[p], delta[p], kbuf[p], ALU.mult).then_inc(dv_ok, 1)
                    if exists(n - 1):
                        wait(pool, l1_ok, n)
                        wait(pool, l2_ok, n)
                        nc.gpsimd.tensor_tensor(den[1 - p], den[1 - p], rbuf[1 - p], ALU.add).then_inc(s_ok, 1)
                    if exists(n):
                        wait(pool, df_ok, n + 1)
                        wait(pool, db_ok, n + 1)
                        nc.gpsimd.tensor_tensor(den[p], den[p], db, ALU.add).then_inc(sum1_ok, 1)
                        wait(pool, sum1_ok, n + 1)
                        nc.gpsimd.tensor_tensor(den[p], den[p], delta[p], ALU.add).then_inc(den_ok, 1)

                over_tiles(pool, body, 1)

            @block.tensor
            def _(pe):
                pe.wait_ge(c_id, 8)

                def body(n, p):
                    def numerator(v, have, used, k):
                        wait(pe, have, n + 1)
                        for h in range(2):
                            cols = slice(512 * h, 512 * h + 512)
                            last = nc.tensor.matmul(ps_num[p][:, cols], ident[:], v[:, cols], start=(k == 0),
                                                    stop=(k == 2), skip_group_check=True)
                        if used:
                            last.then_inc(used, 1)

                    if exists(n - 2):
                        wait(pe, x0_ok, n - 1)
                        wait(pe, nat_ev, n - 2)
                        for tc in range(NC):
                            last = nc.tensor.transpose(ps_nat[:, tc * P:(tc + 1) * P], x0T[:, tc * P:(tc + 1) * P],
                                                       ident[:])
                        last.then_inc(nat_ok, 1)
                    if exists(n):
                        numerator(kbuf[p], dv_ok, dv_used, 0)
                    if exists(n - 2):
                        wait(pe, sq_ok, n - 1)
                        wait(pe, cws_ok, n - 1)
                        wait(pe, lg_add, n - 2)
                        for k, (w, v) in enumerate(((cws[:, p, :], x0T), (sumsq_w[:], sq))):
                            for q in range(Q):
                                last = nc.tensor.matmul(ps_lg[32 * q:32 * q + 32, 0:TQ], w,
                                                        v[:, q * TQ:(q + 1) * TQ], start=(k == 0), stop=(k == 1))
                        last.then_inc(lg_ok, 1)
                    if exists(n):
                        numerator(nf, nf_ok, None, 1)
                        numerator(nb, nb_ok, num_ok, 2)

                over_tiles(pe, body, 2)

        CH = C // 2
        ring = [cut(at, 4096).rearrange("p (a c) -> p a c", a=4) for at in (0, 4096, 10240)]
        lgT, repl, ew = cut(10240, 1032), cut(11272, 1032), cut(12304, T)
        WTz = cut(8192, 1024).rearrange("p (t b s) -> p t b s", t=NC, b=B)
        Xb = cut(9216, C)
        XbT = cut(14336, NC * BS).rearrange("p (c s) -> p c s", c=NC)
        wbb, tsum = cut(14848, CH), cut(15360, CH)
        nat = [cut(14336, CH), cut(14848, CH)]
        kkz = cut(8192, 1024).rearrange("p (h b s) -> p h b s", h=HP, b=B)
        vvz = cut(9216, 1024).rearrange("p (h b s) -> p h b s", h=HP, b=B)
        stageA = [cut(14336 + 512 * i, 512) for i in range(4)]
        stageB = [cut(8192, 1024)[64 * i:64 * i + 64, :] for i in (0, 1)]
        Amat = cut(10240, 4096).rearrange("p (i h x) -> p i h x", i=2, h=HP)
        Bmat = [cut(at, 2048).rearrange("p (i x) -> p i x", i=2) for at in (14336, 0)]
        sbias = sb("sbias", [P, 2, HS])
        bias_in = [sem("score_bias_in_0"), sem("score_bias_in_1")]
        lognat = cut(16384, NC * BS).rearrange("p (t x) -> p t x", t=NC)
        wsT = cut(16384, NC * BS).rearrange("p (c x) -> p c x", c=NC)
        ws, npb = cut(16896, CH), cut(17920, C)
        brows = cut(17408, CH)
        sbrow, obrow = [brows[0:1, :], brows[32:33, :]], [brows[64:65, :], brows[96:97, :]]

        head_sems, tail_sems = {}, {}

        def stage_sem(held, name):
            if name not in held:
                held[name] = sem(name)
            return held[name]

        def load_bias(sp, t, b):
            wait(sp, bias_in[t], 16 * b)
            sp.dma_start(sbias[:, b % 2, :], sb_d[b:b + 1, :, :].rearrange("o h r -> o (h r)").broadcast_to([P, HS]))\
                .then_inc(bias_in[t], 16)

        xTb = [cut(2048 + 1024 * i, 1024).rearrange("p (c t) -> p c t", c=NC) for i in (0, 1)]
        xT_in = [[sem(f"xT_in_{t}_even"), sem(f"xT_in_{t}_odd")] for t in range(2)]

        def load_x(sp, t, b, tc, m, p):
            if t == 0:
                src = x0T_d[b * NC:(b + 1) * NC, :, bass.ds(tc * P, P)].rearrange("c p t -> p c t")
            else:
                src = x1T_d[m, :, :].rearrange("p (c t) -> p c t", c=NC)
            sp.dma_start(xTb[p], src).then_inc(xT_in[t][p], 16)

        def head(t):
            def hsem(name):
                return stage_sem(head_sems, f"head_{name}")

            c_in, st_s = hsem("rows_in"), hsem("bias_out")
            w_in = [hsem(f"weights_in_{i}") for i in range(3)]
            wo_in = [hsem(f"wo_in_{i}") for i in range(4)]
            st_a = [hsem(f"A_out_{i}") for i in range(4)]
            st_b = [hsem("B_out_even"), hsem("B_out_odd")]
            if t == 0:
                lgt_ps, nat_rstd, nat_ln, lognat_ok = (
                    hsem(x) for x in ("lgt_ps", "nat_rstd", "nat_ln", "lognat_ok"))
            lgT_ps, lgT_ok, dtop, sel_ok, repl_ok = (hsem(x) for x in ("lgT_ps", "lgT_ok", "top", "sel", "repl"))
            e4_ok, e_ok, mask_ok, w_ok, wt_ps = (hsem(x) for x in ("e4", "e", "mask", "W", "WT_ps"))
            wtz0, wtz_ok, xb_ps, xb_a, xb_d = (hsem(x) for x in ("WTz0", "WTz", "Xb_ps", "Xb_act", "Xb_dve"))
            xbt_ps, xbt_ok, wr_ps, t1_ok, t2_ok = (hsem(x) for x in ("XbT_ps", "XbT", "write_ps", "t1", "t2"))
            ssq_ok, ln_ok, rs_ok, ws_ok, wst_ps = (hsem(x) for x in ("ssq", "ln", "rstd", "ws", "wsT_ps"))
            wsT_ok, kk_ps, kz, kk_ok, vv_ps, vv_ok = (hsem(x) for x in ("wsT", "kk_ps", "kkz0", "kk", "vv_ps", "vv"))
            ss_ps, kn_ok, vn_ok, kt_ps, vt_ps = (hsem(x) for x in ("ssq_ps", "kk_nat", "vv_nat", "kkT_ps", "vvT_ps"))
            prod_ps, ev_a, ev_d, sb_ps, sb_ok = (hsem(x) for x in ("prod_ps", "ev_act", "ev_dve", "sb_ps", "sb"))
            psA, psB, psX, ps3 = banks[0], banks[1], banks[3], banks[2]
            psC, psK = ps3[:, 0:512], ps3[:, 512:1024]
            psW, psT = psB[:, 0:512], psB[:, 512:1024]

            def prod(i):
                return banks[(0, 3)[i % 2] if i < HP else (0, 3, 1, 2)[i % 4]]

            def wait_product(eng, i, copies=3):
                if i >= 0:
                    eng.wait_ge(ev_d if i % 2 else ev_a,
                                2 * (i // 2 + 1) if i < HP else HP + 3 * ((i - HP) // 2) + copies)

            def keep_warm(ps, n):
                for _ in range(n):
                    nc.tensor.matmul(ps[:, 0:512], ident[:], xres[:, 0, 0:4, :], start=True, stop=True)

            with nc.Block() as block:
                @block.sync
                def _(sp):
                    def piece(slot, w, i):
                        sp.dma_start(ring[slot], w[:, 4 * i:4 * i + 4, :]).then_inc(w_in[slot], 16)

                    piece(0, wr_T, 0)
                    piece(1, wr_T, 1)
                    if t == 0:
                        sp.wait_ge(lgt_ps, 1)
                        for h in range(2):
                            half = slice(CH * h, CH * h + CH)
                            sp.dma_start(obrow[h], wo_b[half].rearrange("(o c) -> o c", o=1)).then_inc(c_in, 16)
                            sp.dma_start(ws[64 * h:64 * h + 64, :], work_t[:, half]).then_inc(c_in, 16)
                        sp.dma_start(npb, npost.rearrange("(o c) -> o c", o=1).broadcast_to([P, C])).then_inc(c_in, 16)
                    for h in range(2):
                        sp.dma_start(wbb[64 * h:64 * h + 64, :], wr_b[CH * h:CH * h + CH]
                                     .rearrange("(o c) -> o c", o=1).broadcast_to([BS, CH])).then_inc(c_in, 16)
                    for slot, w, i, free, count in ((2, wk_T, 0, wt_ps, 1), (0, wk_T, 1, wr_ps, 1),
                                                    (1, wv_T, 0, wr_ps, 2), (2, wv_T, 1, kk_ps, 1),
                                                    (0, wq, 0, kk_ps, 2), (1, wq, 1, vv_ps, 1)):
                        sp.wait_ge(free, count)
                        piece(slot, w, i)
                    sp.wait_ge(sb_ok, 2)
                    for h in range(2):
                        sp.dma_start(sb_d[:, 4 * h:4 * h + 4, :].rearrange("(o b) h s -> o h b s", o=1),
                                     sbrow[h].rearrange("o (h b s) -> o h b s", h=4, b=B)).then_inc(st_s, 16)
                    for i in range(HP):
                        wait_product(sp, i)
                        sp.dma_start(A_d[2:B, i, :, :].rearrange("b p x -> p b x"),
                                     stageA[i % 4].rearrange("p (b x) -> p b x", b=2)).then_inc(st_a[i % 4], 16)
                        if i % 2:
                            sp.dma_start(ring[i // 4][:, i % 4 - 1:i % 4 + 1, :], wo_T[:, i - 1:i + 1, :])\
                                .then_inc(wo_in[i // 2], 16)
                    sp.wait_ge(st_s, 32)
                    load_bias(sp, t, 0)
                    for i in range(HP, 2 * HP):
                        k, r32 = (i - HP) // 4, (i - HP) % 4 * 32
                        wait_product(sp, i, 1)
                        for b in range(2, B):
                            sp.dma_start(Bm_d[b, k, r32:r32 + 32, :], stageB[i % 2][32 * b - 64:32 * b - 32, :])\
                                .then_inc(st_b[i % 2], 16)
                        if i == HP + 3:
                            load_bias(sp, t, 1)
                            for m in range(2):
                                load_x(sp, t, 0, m, m, m)
                    for i in range(4):
                        sp.wait_ge(st_a[i], 16 * 2)
                    sp.wait_ge(st_b[0], 16 * 8)
                    sp.wait_ge(st_b[1], 16 * 8)
                    sp.wait_ge(bias_in[t], 16 * 2)

                @block.tensor
                def _(pe):
                    if t == 0:
                        for i in range(2 * B):
                            last = nc.tensor.transpose(psA[:, i * P:(i + 1) * P],
                                                       lgacc[:, i // 2, (i % 2) * P:(i % 2 + 1) * P], ident[:])
                        last.then_inc(lgt_ps, 1)
                        pe.wait_ge(lognat_ok, B)
                    for c in range(NC):
                        last = nc.tensor.transpose(psB[0:BS, c * P:(c + 1) * P], lognat[:, c, :], ident[:])
                    last.then_inc(lgT_ps, 1)
                    keep_warm(psX, 5)
                    pe.wait_ge(w_ok, 1)
                    for c in range(NC):
                        last = nc.tensor.transpose(psC[:, c * BS:(c + 1) * BS], ew[0:BS, c * P:(c + 1) * P],
                                                   ident[0:BS, 0:BS])
                    last.then_inc(wt_ps, 1)
                    pe.wait_ge(wtz_ok, 1)
                    for c in range(NC):
                        for h in range(2):
                            for b in range(B):
                                last = nc.tensor.matmul(
                                    psX[32 * b:32 * b + 32, 512 * h:512 * h + 512], WTz[:, c, b, :],
                                    xres[:, b * NC + 4 * h:b * NC + 4 * h + 4, c, :],
                                    start=(c == 0), stop=(c == NC - 1), skip_group_check=True)
                    last.then_inc(xb_ps, 1)
                    pe.wait_ge(xb_a, 1)
                    pe.wait_ge(xb_d, 1)
                    for c in range(NC):
                        last = nc.tensor.transpose(psA[:, c * P:(c + 1) * P], Xb[:, c * P:(c + 1) * P], ident[:])
                    last.then_inc(xbt_ps, 1)
                    pe.wait_ge(xbt_ok, 1)

                    def project(ps, xT, i, slot, done):
                        for c in range(4 * i, 4 * i + 4):
                            for q in range(Q):
                                last = nc.tensor.matmul(
                                    ps[32 * q:32 * q + 32, :], xT[:, c, 32 * (q % 2):32 * (q % 2) + 32],
                                    ring[slot][:, c % 4, CH * (q // 2):CH * (q // 2) + CH],
                                    start=(c == 0), stop=(c == NC - 1), skip_group_check=True)
                        last.then_inc(done, 1)

                    def unfold(ps, src, done):
                        for j in range(4):
                            last = nc.tensor.transpose(ps[:, j * P:(j + 1) * P], src[:, j * P:(j + 1) * P], ident[:])
                        last.then_inc(done, 1)

                    for i in range(2):
                        pe.wait_ge(w_in[i], 16)
                        project(psW, XbT, i, i, wr_ps)
                    keep_warm(psX, 1)
                    pe.wait_ge(ssq_ok, 1)
                    for h in range(2):
                        for k in range(2):
                            last = nc.tensor.matmul(psT[64 * h:64 * h + 64, 0:1], ident[:, 64 * k:64 * k + 64],
                                                    hstat[:, 0:1], start=(k == 0), stop=(k == 1),
                                                    skip_group_check=True)
                    last.then_inc(ss_ps, 1)
                    keep_warm(psX, 1)
                    pe.wait_ge(ws_ok, 2)
                    unfold(psC, ws, wst_ps)
                    pe.wait_ge(wsT_ok, 1)
                    for i, slot, loads in ((0, 2, 1), (1, 0, 2)):
                        pe.wait_ge(w_in[slot], 16 * loads)
                        project(psK, wsT, i, slot, kk_ps)
                    for i, slot in ((0, 1), (1, 2)):
                        pe.wait_ge(w_in[slot], 16 * 2)
                        project(psC, wsT, i, slot, vv_ps)
                        if i == 0:
                            pe.wait_ge(kn_ok, 1)
                            unfold(psT, nat[0], kt_ps)
                    pe.wait_ge(kk_ok, 4)
                    for hp in range(HP):
                        r0 = 32 * (hp // 4)
                        last = nc.tensor.matmul(psK[r0:r0 + 1, hp % 4 * P:(hp % 4 + 1) * P], bqc[:, hp:hp + 1],
                                                kkz[:, hp, :, :], start=True, stop=True)
                    last.then_inc(sb_ps, 1)
                    pe.wait_ge(vn_ok, 1)
                    unfold(psW, nat[1], vt_ps)
                    for i in range(2 * HP):
                        hp, slot = i % HP, i % HP // 4
                        ps = prod(i)
                        if i < HP + 2:
                            wait_product(pe, i - 2)
                        elif i >= HP + 4:
                            wait_product(pe, i - 4)
                        if i < HP:
                            if i % 4 == 0:
                                pe.wait_ge(w_in[slot], 16 * 3)
                            for c in range(NC):
                                last = nc.tensor.matmul(ps[:, c * P:(c + 1) * P],
                                                        ring[slot][:, hp % 4, c * P:(c + 1) * P], kkz[:, hp, :, :],
                                                        start=True, stop=True)
                        else:
                            pe.wait_ge(vv_ok, 4)
                            if i % 2 == 0:
                                pe.wait_ge(wo_in[hp // 2], 16)
                            for h in range(2):
                                cols = slice(512 * h, 512 * h + 512)
                                last = nc.tensor.matmul(ps[:, cols], vvz[:, hp, :, :], ring[slot][:, hp % 4, cols],
                                                        start=True, stop=(hp > 0))
                                if hp == 0:
                                    last = nc.tensor.matmul(ps[:, cols], head0_row[h], obrow[h],
                                                            start=False, stop=True)
                        last.then_inc(prod_ps, 1)
                    wait_product(pe, 2 * HP - 4)
                    keep_warm(prod(2 * HP - 4), 3)

                def copy_product(eng, copy, i):
                    eng.wait_ge(prod_ps, i + 1)
                    done, ps = ev_d if i % 2 else ev_a, prod(i)
                    if i < HP:
                        new = ps[:, :].rearrange("p (c b r) -> p b c r", c=NC, b=B)
                        copy(Amat[:, :, i, :].rearrange("p b (c r) -> p b c r", c=NC), new[:, 0:2, :, :])\
                            .then_inc(done, 1)
                        wait(eng, st_a[i % 4], 16 * (i // 4))
                        copy(stageA[i % 4].rearrange("p (b c r) -> p b c r", b=2, c=NC), new[:, 2:B, :, :])\
                            .then_inc(done, 1)
                    else:
                        k, r32 = (i - HP) // 4, (i - HP) % 4 * 32
                        wait(eng, st_b[i % 2], 32 * ((i - HP) // 2))
                        copy(stageB[i % 2], ps[64:P, :]).then_inc(done, 1)
                        if i < HP + 2:
                            for j in range(4):
                                eng.wait_ge(st_a[j], 16 * 2)
                        for b in range(2):
                            copy(Bmat[k][r32:r32 + 32, b, :], ps[32 * b:32 * b + 32, :]).then_inc(done, 1)

                @block.gpsimd
                def _(pool):
                    for s in cond_sems if t == 0 else tail_sems.values():
                        pool.sem_clear(s)

                @block.scalar
                def _(act):
                    nc.scalar.preload_act_table_set("natural_log_exp_and_others")
                    if t == 0:
                        act.wait_ge(lgt_ps, 1)
                        ss = psA[:, :].rearrange("p (g q r) -> p g q r", g=2 * B, q=Q)[:, :, :, S]
                        sm = small[:].rearrange("p (g q) -> p g q", g=2 * B)
                        nc.scalar.activation(sm, ss, ACT.Ln, bias=tiny[:, 2:3], scale=1.0 / C).then_inc(nat_ln, 1)
                        act.wait_ge(nat_ln, 1)
                        nc.scalar.activation(small[:], small[:], ACT.Exp, scale=-0.5).then_inc(nat_rstd, 1)
                    act.wait_ge(lgT_ps, 1)
                    nc.scalar.activation(lgT[0:BS, 0:T], psB[0:BS, :], ACT.Identity, bias=cbcol[:]).then_inc(lgT_ok, 1)
                    act.wait_ge(sel_ok, 2)
                    nc.scalar.activation(top8[:, 16:20], top8[:, 0:4], ACT.Exp, bias=top8[:, 20:21],
                                         accum_out=top8[:, 21:22]).then_inc(e4_ok, 1)
                    nc.scalar.activation(ew[0:BS, :], lgT[0:BS, 0:T], ACT.Exp, bias=top8[:, 20:21]).then_inc(e_ok, 1)
                    act.wait_ge(xb_ps, 1)
                    nc.scalar.activation(Xb[:, 0:512], psX[:, 0:512], ACT.Copy).then_inc(xb_a, 1)
                    act.wait_ge(t2_ok, 1)
                    nc.scalar.activation(nat[0], tsum, ACT.Square, accum_out=hstat[:, 0:1]).then_inc(ssq_ok, 1)
                    act.wait_ge(ss_ps, 1)
                    nc.scalar.activation(hstat[:, 1:2], psT[:, 0:1], ACT.Ln, bias=tiny[:, 2:3], scale=1.0 / C)\
                        .then_inc(ln_ok, 1)
                    act.wait_ge(ln_ok, 1)
                    nc.scalar.activation(hstat[:, 2:3], hstat[:, 1:2], ACT.Exp, scale=-0.5).then_inc(rs_ok, 1)
                    act.wait_ge(kk_ps, 2)
                    nc.scalar.activation(nat[0], psK, ACT.Copy).then_inc(kn_ok, 1)
                    act.wait_ge(vv_ps, 2)
                    nc.scalar.activation(nat[1], psC, ACT.Copy).then_inc(vn_ok, 1)
                    for i in range(0, 16, 2):
                        copy_product(act, lambda o, x: nc.scalar.activation(o, x, ACT.Copy), i)

                @block.vector
                def _(dve):
                    nc.vector.memset(WTz, 0.0).then_inc(wtz0, 1)
                    nc.vector.memset(lgT[0:BS, T:T + 4], BIG).then_inc(wtz0, 1)
                    if t == 0:
                        dve.wait_ge(nat_rstd, 1)
                        for b in range(B):
                            src = psA[:, b * 256:(b + 1) * 256].rearrange("p (h q r) -> p h q r", h=2, q=Q)
                            rst = small[:, b * 8:(b + 1) * 8].rearrange("p (h q o) -> p h q o", h=2, o=1)
                            dst = lognat[:, :, b * S:(b + 1) * S].rearrange("p (q h) s -> p h q s", h=2)
                            nc.vector.tensor_tensor(dst, src[:, :, :, 0:S], rst.broadcast_to([P, 2, Q, S]),
                                                    ALU.mult).then_inc(lognat_ok, 1)
                    dve.wait_ge(lgT_ok, 1)
                    nc.vector.max(top8[:, 0:8], lgT[0:BS, 0:T]).then_inc(dtop, 1)
                    dve.wait_ge(dtop, 1)
                    nc.vector.tensor_copy(top8[:, 8:12], top8[:, 0:4]).then_inc(sel_ok, 1)
                    nc.vector.tensor_scalar(top8[:, 20:21], top8[:, 0:1], -1.0, None, ALU.mult).then_inc(sel_ok, 1)
                    dve.wait_ge(sel_ok, 1)
                    dve.wait_ge(wtz0, 2)
                    nc.vector.match_replace(repl[0:BS, 0:T + 4], top8[:, 8:16], lgT[0:BS, 0:T + 4], -BIG)\
                        .then_inc(repl_ok, 1)
                    dve.wait_ge(repl_ok, 1)
                    nc.vector.tensor_tensor(repl[0:BS, 0:T], repl[0:BS, 0:T], lgT[0:BS, 0:T], ALU.not_equal)\
                        .then_inc(mask_ok, 1)
                    dve.wait_ge(e4_ok, 1)
                    nc.vector.reciprocal(top8[:, 22:23], top8[:, 21:22]).then_inc(mask_ok, 1)
                    dve.wait_ge(mask_ok, 2)
                    dve.wait_ge(e_ok, 1)
                    nc.vector.scalar_tensor_tensor(ew[0:BS, :], repl[0:BS, 0:T], top8[:, 22:23], ew[0:BS, :],
                                                   ALU.mult, ALU.mult).then_inc(w_ok, 1)
                    dve.wait_ge(wt_ps, 1)
                    nc.vector.tensor_copy(WTz[:, :, :, 0:S], psC.rearrange("p (t b s) -> p t b s", t=NC, b=B))\
                        .then_inc(wtz_ok, 1)
                    dve.wait_ge(c_in, 16 * (7 if t == 0 else 2))
                    nc.vector.tensor_tensor(wbb, wbb, ws, ALU.add).then_inc(t1_ok, 1)
                    dve.wait_ge(xb_ps, 1)
                    nc.vector.tensor_copy(Xb[:, 512:1024], psX[:, 512:1024]).then_inc(xb_d, 1)
                    dve.wait_ge(xbt_ps, 1)
                    nc.vector.tensor_copy(XbT.rearrange("p c (b s) -> p c b s", b=B),
                                          psA[:, :].rearrange("p (c b r) -> p c b r", c=NC, b=B)[:, :, :, 0:S])\
                        .then_inc(xbt_ok, 1)
                    nc.vector.memset(cut(8192, 2048), 0.0).then_inc(kz, 1)
                    dve.wait_ge(wr_ps, 2)
                    dve.wait_ge(t1_ok, 1)
                    nc.vector.tensor_tensor(tsum, psW, wbb, ALU.add).then_inc(t2_ok, 1)
                    dve.wait_ge(rs_ok, 1)
                    for h in range(2):
                        rows = slice(64 * h, 64 * h + 64)
                        nc.vector.scalar_tensor_tensor(ws[rows, :], tsum[rows, :], hstat[rows, 2:3],
                                                       npb[rows, CH * h:CH * h + CH], ALU.mult, ALU.mult)\
                            .then_inc(ws_ok, 1)
                    dve.wait_ge(wst_ps, 1)
                    nc.vector.tensor_copy(wsT.rearrange("p (h j) x -> p j h x", h=2),
                                          psC.rearrange("p (j h x) -> p j h x", j=4, h=2)).then_inc(wsT_ok, 1)
                    dve.wait_ge(kz, 1)
                    for ps, z, bias, have, done in ((psT, kkz, bkc, kt_ps, kk_ok), (psW, vvz, bvc, vt_ps, vv_ok)):
                        dve.wait_ge(have, 1)
                        for h in range(2):
                            for e in range(2):
                                rows = slice(64 * e, 64 * e + 64)
                                nc.vector.tensor_tensor(
                                    z[rows, 4 * h:4 * h + 4, :, S * e:S * e + S],
                                    ps[rows, :].rearrange("p (j g b s) -> p j g b s", j=4, g=2, b=B)[:, :, h, :, :],
                                    bias[rows, 4 * h:4 * h + 4].rearrange("p (h o i) -> p h o i", o=1, i=1)
                                    .broadcast_to([64, 4, B, S]), ALU.add).then_inc(done, 1)
                        if z is kkz:
                            dve.wait_ge(sb_ps, 1)
                            for h in range(2):
                                nc.vector.tensor_copy(sbrow[h], psK[32 * h:32 * h + 1, :]).then_inc(sb_ok, 1)
                    for i in range(1, 16, 2):
                        copy_product(dve, nc.vector.tensor_copy, i)

        x1s = [cut(4096 + 1024 * i, 1024) for i in (0, 1)]
        y = cut(6144, C)
        sc = [cut(7168 + 256 * i, 256) for i in (0, 1)]
        att, attT = cut(7680, 256), cut(7936, 256)
        x1T, lp = cut(8192, C), cut(9216, P)
        xo = [cut(8192, C), cut(9216, C)]
        junks = [cut(9344, 512).bitcast(bf16), cut(16384, 512).bitcast(bf16)]
        stat = sb("stat", [P, 8])
        mx, den16 = sb("mx", [P, H]), sb("den16", [P, H])

        def tail(t):
            first = t == 0
            junk = junks[t]

            def tsem(name):
                return stage_sem(tail_sems, f"tail_{name}")

            x1_out, xo_in = (
                [tsem(f"{v}_even"), tsem(f"{v}_odd")] for v in ("x1_out", "xo_in"))
            sc_ps, mx_ok, sub_ok, e_ok, sum_ok, rc_ok, att_ok = (
                tsem(v) for v in ("scores_ps", "max", "sub", "exp", "sum", "rcp", "att"))
            bias_ok, mat_in = tsem("bias"), tsem("matrices_in")
            at_ps, at_ev, o_ps, y_ok, ssq_ok, ln_ok, rs_ok, x1_ok = (
                tsem(v) for v in ("attT_ps", "attT", "out_ps", "y", "ssq", "ln", "rstd", "x1"))
            if first:
                x1T_out, xt_ps, xt_ev, ssq2_ok, ln2_ok, rs2_ok, l_ps, lp_ok, l2_ps, l_ok = (
                    tsem(v) for v in ("x1T_out", "x1T_ps", "x1T", "ssq2", "ln2", "rstd2", "l_ps", "lp",
                                      "l2_ps", "logits"))
            else:
                fin = tsem("final")
            ps_s = [banks[0][:, 0:256], banks[0][:, 512:768]]
            ps_at, ps_l = banks[1][:, 0:256], banks[1][:, 512:640]
            ps_l2 = banks[1][:, 640:656]
            ps_o, ps_x = banks[2], banks[3]

            with nc.Block() as block:
                @block.sync
                def _(sp):
                    def store(m, p):
                        if first:
                            wait(sp, x1_ok, m + 1)
                            sp.dma_start(xres[:, bass.ds(m // NC * NC, NC), m % NC, :],
                                         x1s[p].rearrange("p (c x) -> p c x", c=NC)).then_inc(x1_out[p], 16)
                            wait(sp, xt_ev, m + 1)
                            sp.dma_start(x1T_d[m, :, :], x1T).then_inc(x1T_out, 16)
                        else:
                            wait(sp, fin, m + 1)
                            sp.dma_start(out[m, :, :], x1s[p]).then_inc(x1_out[p], 16)

                    def load_residual(m, p):
                        if not first:
                            wait(sp, fin, m - 1)
                            sp.dma_start(xo[p], x[m, :, :]).then_inc(xo_in[p], 16)

                    def step(b, tc, m, p):
                        if not (isinstance(m, int) and m < 2):
                            wait(sp, sc_ps, m - 1)
                            load_x(sp, t, b, tc, m, p)
                        if exists(m - 4):
                            store(m - 4, p)
                        if exists(m - 2):
                            load_residual(m - 2, p)

                    for b in range(B):
                        if b == 0:
                            for tc in range(4):
                                step(0, tc, tc, tc % 2)
                        else:
                            with sp.Fori(0, 2) as j:
                                for p in range(2):
                                    step(b, j * 2 + p, j * 2 + (b * NC + p), p)
                        for tc in range(4, NC):
                            if 2 <= b + 1 < B:
                                i, part = (b + 1) % 2, tc % 2
                                if tc == 4:
                                    wait(sp, o_ps, NC * b)
                                    wait(sp, mat_in, 64 * (b - 1))
                                if tc < 6:
                                    sp.dma_start(Amat[:, i, 4 * part:4 * part + 4, :],
                                                 A_d[b + 1, 4 * part:4 * part + 4, :, :].rearrange("h p x -> p h x"))\
                                        .then_inc(mat_in, 16)
                                else:
                                    sp.dma_start(Bmat[part][:, i, :], Bm_d[b + 1, part, :, :]).then_inc(mat_in, 16)
                            step(b, tc, b * NC + tc, tc % 2)
                        if 2 <= b + 1 < B:
                            sp.wait_ge(mat_in, 64 * b)
                            load_bias(sp, t, b + 1)
                    for m in range(NT - 4, NT):
                        store(m, m % 2)
                        if m + 2 < NT:
                            load_residual(m + 2, m % 2)
                    for p in range(2):
                        sp.wait_ge(x1_out[p], 16 * NT // 2)
                    if first:
                        sp.wait_ge(x1T_out, 16 * NT)

                @block.tensor
                def _(pe):
                    def scores(m, p, part):
                        i = m // NC % 2
                        if part == 0:
                            wait(pe, bias_in[t], (m // NC + 1) * 16)
                            wait(pe, xT_in[t][p], (m // 2 + 1) * 16)
                            wait(pe, bias_ok, m - 1)
                        for c in range(4 * part, 4 * part + 4):
                            last = nc.tensor.matmul(ps_s[p], xTb[p][:, c, :], Amat[:, i, :, c * 32:c * 32 + 32],
                                                    start=(c == 0), stop=(c == NC - 1))
                        if part == 1:
                            last.then_inc(sc_ps, 1)

                    def body(m, p):
                        if exists(m + 1):
                            scores(m + 1, 1 - p, 0)
                        if exists(m):
                            wait(pe, att_ok, m + 1)
                            wait(pe, at_ev, m)
                            for k in range(2):
                                last = nc.tensor.transpose(ps_at[:, k * P:(k + 1) * P], att[:, k * P:(k + 1) * P],
                                                           ident[:])
                            last.then_inc(at_ps, 1)
                        if exists(m + 1):
                            scores(m + 1, 1 - p, 1)
                        if exists(m):
                            i = m // NC % 2
                            wait(pe, at_ev, m + 1)
                            wait(pe, y_ok, m)
                            for k in range(2):
                                for h in range(2):
                                    cols = slice(512 * h, 512 * h + 512)
                                    last = nc.tensor.matmul(ps_o[:, cols], attT[:, k * P:(k + 1) * P],
                                                            Bmat[k][:, i, cols], start=(k == 0), stop=(k == 1),
                                                            skip_group_check=True)
                            last.then_inc(o_ps, 1)
                        if first and exists(m - 2):
                            wait(pe, xt_ev, m - 1)
                            wait(pe, l_ok, m - 2)
                            for c in range(NC):
                                q = c % Q
                                last = nc.tensor.matmul(ps_l[32 * q:32 * q + 32, :], cwz[:, c, :],
                                                        x1T[:, c * P:(c + 1) * P], start=(c < Q), stop=(c >= Q),
                                                        skip_group_check=True)
                            last.then_inc(l_ps, 1)
                        if first and exists(m - 1):
                            wait(pe, x1_ok, m)
                            for c in range(NC):
                                last = nc.tensor.transpose(ps_x[:, c * P:(c + 1) * P],
                                                           x1s[1 - p][:, c * P:(c + 1) * P], ident[:])
                            last.then_inc(xt_ps, 1)
                        if first and exists(m - 2):
                            wait(pe, lp_ok, m - 1)
                            nc.tensor.matmul(ps_l2, lp, fold[:], start=True, stop=True).then_inc(l2_ps, 1)

                    scores(0, 0, 0)
                    scores(0, 0, 1)
                    over_tiles(pe, body, 2 if first else 0)

                @block.vector
                def _(dve):
                    def submax(m, p):
                        s3 = sc[p].rearrange("p (h s) -> p h s", h=H)
                        wait(dve, sc_ps, m + 1)
                        wait(dve, bias_in[t], (m // NC + 1) * 16)
                        nc.vector.tensor_tensor(sc[p], ps_s[p], sbias[:, m // NC % 2, :], ALU.add)\
                            .then_inc(bias_ok, 1)
                        wait(dve, bias_ok, m + 1)
                        nc.vector.tensor_reduce(mx[:], s3, AXX, ALU.max).then_inc(mx_ok, 1)
                        wait(dve, mx_ok, m + 1)
                        nc.vector.tensor_tensor(s3, s3,
                                                mx[:].rearrange("p (h o) -> p h o", o=1).broadcast_to([P, H, S]),
                                                ALU.subtract).then_inc(sub_ok, 1)

                    def body(m, p):
                        if exists(m):
                            e3 = sc[p].rearrange("p (h s) -> p h s", h=H)
                            wait(dve, e_ok, m + 1)
                            nc.vector.tensor_reduce(den16[:], e3, AXX, ALU.add).then_inc(sum_ok, 1)
                            wait(dve, sum_ok, m + 1)
                            nc.vector.reciprocal(den16[:], den16[:]).then_inc(rc_ok, 1)
                            wait(dve, rc_ok, m + 1)
                            wait(dve, at_ps, m)
                            nc.vector.tensor_tensor(att.rearrange("p (h s) -> p h s", h=H), e3,
                                                    den16[:].rearrange("p (h o) -> p h o", o=1)
                                                    .broadcast_to([P, H, S]), ALU.mult).then_inc(att_ok, 1)
                        if first and exists(m - 3):
                            n = m - 3
                            wait(dve, l2_ps, m - 2)
                            wait(dve, rs2_ok, m - 2)
                            nc.vector.tensor_scalar(lognat[:, n % NC, bass.ds(n // NC * S, S)], ps_l2,
                                                    stat2[1 - p][:, 2:3],
                                                    None, ALU.mult).then_inc(l_ok, 1)
                        if exists(m - 1):
                            n = m - 1
                            wait(dve, o_ps, m)
                            wait(dve, x1_ok, m - 1)
                            nc.vector.tensor_tensor(y.rearrange("p (c x) -> p c x", c=NC),
                                                    ps_o[:, :].rearrange("p (c x) -> p c x", c=NC),
                                                    xres[:, bass.ds(n // NC * NC, NC), n % NC, :],
                                                    ALU.add).then_inc(y_ok, 1)
                        if exists(m + 1):
                            submax(m + 1, 1 - p)
                        if exists(m - 1):
                            wait(dve, rs_ok, m)
                            wait(dve, x1_out[1 - p], (m - 1) // 2 * 16)
                            if first:
                                wait(dve, xt_ps, m - 2)
                                wait(dve, ssq2_ok, m - 2)
                            nc.vector.scalar_tensor_tensor(x1s[1 - p], y, stat[:, 2:3], npb, ALU.mult, ALU.mult)\
                                .then_inc(x1_ok, 1)

                    submax(0, 0)
                    over_tiles(dve, body, 3 if first else 1)

                @block.scalar
                def _(act):
                    nc.scalar.preload_act_table_set("natural_log_exp_and_others")

                    def expo(m, p):
                        wait(act, sub_ok, m + 1)
                        nc.scalar.activation(sc[p], sc[p], ACT.Exp, scale=SCALE).then_inc(e_ok, 1)

                    def body(m, p):
                        if exists(m):
                            wait(act, at_ps, m + 1)
                            wait(act, o_ps, m)
                            nc.scalar.activation(attT, ps_at, ACT.Copy).then_inc(at_ev, 1)
                        if exists(m - 1):
                            wait(act, y_ok, m)
                            nc.scalar.activation(junk, y, ACT.Square, accum_out=stat[:, 0:1]).then_inc(ssq_ok, 1)
                            wait(act, ssq_ok, m)
                            nc.scalar.activation(stat[:, 1:2], stat[:, 0:1], ACT.Ln, bias=tiny[:, 2:3],
                                                 scale=1.0 / C).then_inc(ln_ok, 1)
                            wait(act, ln_ok, m)
                            nc.scalar.activation(stat[:, 2:3], stat[:, 1:2], ACT.Exp, scale=-0.5).then_inc(rs_ok, 1)
                        if exists(m + 1):
                            expo(m + 1, 1 - p)
                        if first and exists(m - 2):
                            wait(act, l_ps, m - 1)
                            nc.scalar.activation(lp, ps_l, ACT.Copy).then_inc(lp_ok, 1)
                        if first and exists(m - 1):
                            q = stat2[1 - p]
                            wait(act, x1_ok, m)
                            wait(act, l_ok, m - 2)
                            nc.scalar.activation(junk, x1s[1 - p], ACT.Square, accum_out=q[:, 0:1])\
                                .then_inc(ssq2_ok, 1)
                            wait(act, ssq2_ok, m)
                            nc.scalar.activation(q[:, 1:2], q[:, 0:1], ACT.Ln, bias=tiny[:, 2:3],
                                                 scale=1.0 / C).then_inc(ln2_ok, 1)
                            wait(act, ln2_ok, m)
                            nc.scalar.activation(q[:, 2:3], q[:, 1:2], ACT.Exp, scale=-0.5).then_inc(rs2_ok, 1)
                            wait(act, xt_ps, m)
                            wait(act, l_ps, m - 1)
                            wait(act, x1T_out, (m - 1) * 16)
                            nc.scalar.activation(x1T, ps_x[:, :], ACT.Copy).then_inc(xt_ev, 1)

                    expo(0, 0)
                    over_tiles(act, body, 2 if first else 1)

                if first:
                    @block.gpsimd
                    def _(pool):
                        for s in head_sems.values():
                            pool.sem_clear(s)
                else:
                    @block.gpsimd
                    def _(pool):
                        def body(m, p):
                            wait(pool, x1_ok, m + 1)
                            wait(pool, xo_in[p], (m // 2 + 1) * 16)
                            nc.gpsimd.tensor_tensor(x1s[p], x1s[p], xo[p], ALU.add).then_inc(fin, 1)

                        over_tiles(pool, body, 0)

        stat2 = [sb("stat_even", [P, 4]), sb("stat_odd", [P, 4])]
        for t in range(2):
            head(t)
            if t == 0:
                cond_ctx.close()
            tail(t)


def kernel(**inputs):
    import numpy as np
    import concourse.bacc as bacc
    from concourse.bass_utils import run_bass_kernel_spmd

    i = {k: np.asarray(v) for k, v in inputs.items()}

    def cols(v, rep=1):
        return np.tile(v.reshape(-1, P).T, (1, rep))

    def chunked(w):
        return w.reshape(-1, P, w.shape[1]).transpose(1, 0, 2)

    ipw, ipb = i["L0_ffn_in_proj_w"], i["L0_ffn_in_proj_b"]
    arrays = {
        "xT": i["x"].transpose(0, 2, 1).reshape(NT, P, T),
        "kT": i["fside_BxSxS_0"].transpose(0, 2, 1).reshape(NT, P, T),
        "x_nat": i["x"].reshape(NT, P, C),
        "cond": i["cond_512"],
        "w_cols": cols(i["L0_cond_w"], B),
        "u_cols": cols(i["L0_cond_u"], B),
        "workspace": np.tile(i["L0_ffn_workspace"], (B, 1)),
        "cw_cols": chunked(i["L0_ffn_compete_w"].T).reshape(P, NC * S),
        "npre_cols": cols(i["L0_ffn_norm_pre_w"]),
        "cb_col": np.tile(i["L0_ffn_compete_b"], B).reshape(BS, 1),
        "wr_T": chunked(i["L0_ffn_write_w"].T),
        "wr_b": i["L0_ffn_write_b"],
        "wq": chunked(ipw[:C]),
        "wk_T": chunked(ipw[C:2 * C].T),
        "wv_T": chunked(ipw[2 * C:].T),
        "bq_cols": cols(ipb[:C]),
        "bk_cols": cols(ipb[C:2 * C]),
        "bv_cols": cols(ipb[2 * C:]),
        "wo_T": chunked(i["L0_ffn_out_proj_w"].T),
        "wo_b": i["L0_ffn_out_proj_b"],
        "npost": i["L0_ffn_norm_post_w"],
    }
    nc = bacc.Bacc("TRN2", target_bir_lowering=False, num_devices=1)
    fed, args = {}, []
    for name, a in arrays.items():
        a = np.ascontiguousarray(a)
        fed[f"in_{name}"] = a
        args.append(nc.dram_tensor(f"in_{name}", a.shape, mybir.dt.from_np(a.dtype), kind="ExternalInput").ap())
    args.append(nc.dram_tensor("out_0", [NT, P, C], fp32, kind="ExternalOutput").ap())
    build(nc, *args)
    r = run_bass_kernel_spmd(nc, [fed], core_ids=[0])
    return r.results[0]["out_0"].reshape(B, T, C)
```
